# Optimizing a Trainium2 kernel written in Bass

```python
import numpy as np
import jax
import jax.numpy as jnp

def _softmax(x, axis=-1):
    return jax.nn.softmax(x, axis=axis)

def _gelu(x):
    return jax.nn.gelu(x, approximate=True)

def _silu(x):
    return jax.nn.silu(x)

def _sigmoid(x):
    return jax.nn.sigmoid(x)

def _layernorm(x, axis=-1, eps=1e-05):
    m = jnp.mean(x, axis=axis, keepdims=True)
    v = jnp.var(x, axis=axis, keepdims=True)
    return (x - m) / jnp.sqrt(v + eps)

def _scatter_add(tgt, idx, src, axis=0):
    return tgt.at[idx].add(src)

def _segment_sum(src, seg, n):
    return jax.ops.segment_sum(src, seg, n)
kernel_name = 'mk_gnn_resnorm_d2_gnn_r64_529e23'

def setup_inputs(seed: int=0):
    np.random.seed(seed)
    _w = jnp.asarray

    def _rec_inputs():
        import jax
        import jax.numpy as jnp
        _gk = jax.random.key(seed)
        x = -0.0005121 + 1.001 * jax.random.normal(jax.random.fold_in(_gk, 1), (100000, 32), jnp.float32)
        src = jax.random.randint(jax.random.fold_in(_gk, 2), (50000,), 0, 100000, jnp.int32)
        dst = jax.random.randint(jax.random.fold_in(_gk, 3), (50000,), 0, 100000, jnp.int32)
        _o = jnp.argsort(dst, stable=True)
        src = src[_o]
        dst = dst[_o]
        edge_attr_32 = -9.77346e-05 + 0.999888 * jax.random.normal(jax.random.fold_in(_gk, 12), (50000, 32), jnp.float32)
        edge_weight = jax.random.uniform(jax.random.fold_in(_gk, 13), (50000,), jnp.float32, 0.0, 1)
        return (x, src, dst, edge_attr_32, edge_weight)
    x, src, dst, edge_attr_32, edge_weight = _rec_inputs()

    def _L0_gnn_setup():
        import jax, jax.numpy as jnp
        import numpy as np
        N_NODES = 100000
        N_EDGES = 25000
        C = 32
        key = jax.random.key(seed)
        k1, k2, k3, k4 = jax.random.split(key, 4)
        signal = jax.random.normal(k1, (N_NODES, C), dtype=jnp.float32)
        weights = jax.random.uniform(k2, (N_EDGES,), dtype=jnp.float32)
        edge_src = jax.random.randint(k3, (N_EDGES,), 0, N_NODES)
        edge_dst = jax.random.randint(k4, (N_EDGES,), 0, N_NODES)
        return {'signal': signal, 'weights': weights, 'edge_src': edge_src, 'edge_dst': edge_dst, 'itr': 10}
    _L0_gnn_all = _L0_gnn_setup()
    _L0_gnn_in = {k: v for k, v in _L0_gnn_all.items() if k in ()}
    del _L0_gnn_all

    def _L1_gnn_setup():
        import jax, jax.numpy as jnp
        import numpy as np
        N_NODES = 100000
        N_EDGES = 25000
        IN_FEATS = 32
        OUT_FEATS = 32
        key = jax.random.key(seed)
        k1, k2, k3, k4, k5, k6 = jax.random.split(key, 6)
        feat = jax.random.normal(k1, (N_NODES, IN_FEATS), dtype=jnp.float32)
        edgeFeat = jax.random.normal(k2, (N_EDGES, IN_FEATS), dtype=jnp.float32)
        limit = float(np.sqrt(6.0 / (IN_FEATS + OUT_FEATS)))
        weight = jax.random.uniform(k3, (IN_FEATS, OUT_FEATS), dtype=jnp.float32, minval=-limit, maxval=limit)
        bias = jnp.zeros((OUT_FEATS,), dtype=jnp.float32)
        src = jax.random.randint(k4, (N_EDGES,), 0, N_NODES, dtype=jnp.int64)
        dst = jax.random.randint(k5, (N_EDGES,), 0, N_NODES, dtype=jnp.int64)
        return {'feat': feat, 'edgeFeat': edgeFeat, 'weight': weight, 'bias': bias, 'src': src, 'dst': dst}
    _L1_gnn_all = _L1_gnn_setup()
    _L1_gnn_in = {k: v for k, v in _L1_gnn_all.items() if k in ('weight', 'bias')}
    del _L1_gnn_all
    return {'x': x, 'src': src, 'dst': dst, 'edge_attr_32': edge_attr_32, 'edge_weight': edge_weight, 'L1_gnn_weight': _L1_gnn_in['weight'], 'L1_gnn_bias': _L1_gnn_in['bias']}

def reference(x, src, dst, edge_attr_32, edge_weight, L1_gnn_weight, L1_gnn_bias):
    import jax
    import jax.numpy as jnp

    def _L0_gnn_ref(signal, weights, edge_src, edge_dst, itr):
        import jax, jax.numpy as jnp
        import numpy as np
        N_NODES = 100000
        N_EDGES = 25000
        C = 32
        n = signal.shape[0]
        sqrt_w = jnp.sqrt(weights)[:, None]

        def step(f, _):
            up = jnp.maximum(f[edge_dst] - f[edge_src], 0.0) * sqrt_w
            inf_norm = jax.ops.segment_max(up, edge_src, num_segments=n)
            inf_norm = jnp.maximum(inf_norm, 0.0)
            return (f + inf_norm, None)
        out, _ = jax.lax.scan(step, signal, None, length=itr)
        return out

    def _L1_gnn_ref(feat, edgeFeat, weight, bias, src, dst):
        import jax, jax.numpy as jnp
        import numpy as np
        N_NODES = 100000
        N_EDGES = 25000
        IN_FEATS = 32
        OUT_FEATS = 32
        N = feat.shape[0]
        ones = jnp.ones(src.shape[0], dtype=feat.dtype)
        out_deg = jnp.maximum(jax.ops.segment_sum(ones, src, num_segments=N), 1.0)
        in_deg = jnp.maximum(jax.ops.segment_sum(ones, dst, num_segments=N), 1.0)
        feat_src = feat * (out_deg ** (-0.5))[:, None]
        msg = feat_src[src] + edgeFeat
        agg = jax.ops.segment_sum(msg, dst, num_segments=N)
        rst = agg @ weight
        rst = rst * (in_deg ** (-0.5))[:, None]
        return rst + bias
    x = _layernorm(x + _L0_gnn_ref(x, edge_weight, src, dst, 10), axis=-1)
    x = _layernorm(x + _L1_gnn_ref(x, edge_attr_32, L1_gnn_weight, L1_gnn_bias, src, dst), axis=-1)
    return x

_drawn_inputs = setup_inputs


def setup_inputs(seed=0):
    import zlib

    import numpy as np

    out = dict(_drawn_inputs(seed))
    spreads = {'L1_gnn_bias': (0.0, 0.1)}
    factors = {}
    for name, (base, spread) in spreads.items():
        noise = np.random.default_rng([zlib.crc32(name.encode()), seed]).standard_normal(out[name].shape)
        drawn = base * np.exp(spread * noise) if base else spread * noise
        out[name] = jnp.asarray(drawn.astype(out[name].dtype))
    for name, factor in factors.items():
        out[name] = (out[name] * factor).astype(out[name].dtype)
    return out
```

```python
from contextlib import ExitStack

import concourse.bass as bass
from concourse import mybir

ALU = mybir.AluOpType
ACT = mybir.ActivationFunctionType
AX = mybir.AxisListType
F32 = mybir.dt.float32
I32 = mybir.dt.int32

P = 128
GC = 28
QUAD = 4
BIG = 3.0e38
KEY_SHIFT = 14
KEY_OFFSET = 512
ITERATIONS = 10
EPS = 1e-5
NEAR = 8
ROWS = 16


class Count:

    def __init__(self, sem, step=1):
        self.sem, self.step, self.n, self.loops = sem, step, 0, []

    def inc(self, instruction):
        self.n += 1
        return instruction.then_inc(self.sem, self.step)

    def value(self):
        v = self.n * self.step
        for i, per in self.loops:
            v = i * (per * self.step) + v
        return v

    def enter(self, i, per):
        self.loops.append((i, per))
        return self.n

    def leave(self, start, trips):
        _, per = self.loops.pop()
        assert self.n - start == per, (self.n - start, per)
        self.n = start + per * trips


def resnorm_gnn(nc, x, src, dst, edge_attr, edge_weight, weight, bias, out, debug=None):
    N, C = x.shape
    E = src.shape[0]
    SIDE = 512
    COLS = -(-E // (P * 2 * GC)) * 2 * GC
    NG = COLS // GC
    SLOTS = P * COLS
    SORTED = P * SIDE
    ER = 100
    EC = E // ER
    LEAD = 16
    KW = LEAD + COLS + LEAD
    WIN = GC + 1
    FLAT = C * WIN
    assert E == ER * EC and EC % QUAD == 0 and EC <= SIDE and NG % 2 == 0 and SLOTS <= SORTED
    assert N + KEY_OFFSET + (SORTED - E) < 1 << 17 and E // QUAD < 1 << KEY_SHIFT
    BLOCK = P * ROWS
    NB = N // BLOCK
    TAILP = (N - NB * BLOCK) // ROWS
    assert NB % 2 == 0 and NB * BLOCK + TAILP * ROWS == N
    AW = C + 1

    def scratch(name, shape, dt):
        kind = "ExternalOutput" if debug and name in debug else "Internal"
        return nc.dram_tensor(name, shape, dt, kind=kind).ap()

    keys_d = scratch("keys_d", [2, LEAD + SORTED], I32)
    rec_d = scratch("rec_d", [E // QUAD, 3 * QUAD], I32)
    map_d = scratch("map_d", [N, 2], I32)
    table_d = [scratch("table0_d", [N + SLOTS, C], F32), scratch("table1_d", [N + SLOTS, C], F32)]
    x1_d = scratch("x1_d", [N, C], F32)
    x1s_d = scratch("x1s_d", [N, C], F32)
    agg_d = scratch("agg_d", [N, AW], F32)

    with ExitStack() as ctx:
        def sb(name, shape, dt):
            return ctx.enter_context(nc.sbuf_tensor(name, shape, dt))

        def psum(name, shape, dt):
            return ctx.enter_context(nc.psum_tensor(name, shape, dt))

        def sem(name):
            return ctx.enter_context(nc.semaphore(name))

        runs = sb("runs", [P, (NG + 1) * FLAT], F32)
        joined = sb("joined", [P, NG * FLAT + 1], F32)
        rows = sb("rows", [P, NG, GC, C], F32)
        stage = sb("stage", [P, 2, GC * AW], F32)
        stage_i = sb("stage_i", [P, 2, GC], I32)
        window = sb("window", [P, FLAT], F32)
        diff = sb("diff", [P, GC, C], F32)
        node = sb("node", [P, 2, KW], F32)
        same = sb("same", [P, 2, COLS], F32)
        other = sb("other", [P, 2, COLS], I32)
        edge_b = sb("edge_b", [P, COLS], I32)
        wgt = sb("wgt", [P, COLS], F32)
        gidx = sb("gidx", [P, COLS], I32)
        clip = sb("clip", [P, COLS], I32)
        last_i = sb("last_i", [P, 2, COLS], I32)
        length = sb("length", [P, 2, COLS], F32)
        slot_i = sb("slot_i", [P, COLS], I32)
        ident = sb("ident", [P, P], F32)
        small = sb("small", [P, 64], F32)
        small_i = sb("small_i", [P, 8], I32)
        match = sb("match", [P, 4, GC, QUAD], F32)
        four = sb("four", [P, QUAD], F32)
        cross = sb("cross", [P, 3, 1 + COLS], F32)
        cross_col = sb("cross_col", [P, 3, C], F32)
        whole = sb("whole", [C, 3, P], F32)
        ends_t = sb("ends_t", [C, 2, P + 1], F32)
        line = sb("line", [1, 4, P + 1], F32)
        longest = sb("longest", [1, 1], I32)
        zero_i = sb("zero_i", [2, LEAD], I32)
        wblk = sb("wblk", [P, P], F32)
        bias_b = sb("bias_b", [P, C], F32)

        def part(tile, start, shape, dt=F32):
            size = 1
            for n in shape:
                size *= n
            v = tile[:, start:start + size]
            if dt is not F32:
                v = v.bitcast(dt)
            if len(shape) == 2:
                v = v.rearrange("p (a b) -> p a b", a=shape[0])
            if len(shape) == 3:
                v = v.rearrange("p (a b c) -> p a b c", a=shape[0], b=shape[1])
            return v

        W2 = 2 * SIDE
        sort_buf = [runs[:, 0:W2], runs[:, W2:2 * W2]]
        turn_buf = [runs[:, 2 * W2:3 * W2], runs[:, 3 * W2:4 * W2]]
        raw_edges = part(runs, 4 * W2, [2, EC], I32)
        raw_w = part(runs, 4 * W2 + 2 * EC, [EC])
        quarter = part(runs, 4 * W2 + 3 * EC, [EC], I32)
        rec = part(runs, 4 * W2 + 4 * EC, [EC // QUAD, 3, QUAD], I32)
        assert 4 * W2 + 7 * EC <= NG * FLAT
        rows_flat = rows[:].rearrange("p g c f -> p (g c f)")
        MR = N // ER
        map_rows = part(rows_flat, 0, [MR, 2], I32)
        AP0, AR = 80, 25
        agg_rows = part(rows_flat, 2 * MR, [AR, AW])
        KA = 2 * MR + AR * AW
        keys = part(rows_flat, KA, [2, KW], I32)
        quad = part(rows_flat, KA + 2 * KW, [2, COLS], I32)
        twin = part(rows_flat, KA + 2 * KW + 2 * COLS, [2, COLS])
        assert KA + 2 * KW + 4 * COLS <= NG * GC * C and N % (AP0 * AR) == 0 and N % ER == 0

        fix = window[:].rearrange("p (f w) -> p f w", w=WIN)

        DW = ROWS * C
        def dense_tiles(tile, h):
            at = h * (6 * DW + 8 * ROWS + ROWS * AW)
            t = {}
            for name, shape, dt in (("x", [ROWS, C], F32), ("f", [ROWS, C], F32), ("y", [ROWS, C], F32),
                                    ("sq", [ROWS, C], F32), ("o", [ROWS, C], F32), ("o2", [ROWS, C], F32),
                                    ("agg", [ROWS, AW], F32), ("map", [ROWS, 2], I32), ("sum", [ROWS], F32),
                                    ("mean", [ROWS], F32), ("var", [ROWS], F32), ("std", [ROWS], F32),
                                    ("rstd", [ROWS], F32), ("deg", [ROWS], F32)):
                n = shape[0] * (shape[1] if len(shape) > 1 else 1)
                t[name] = part(tile, at, shape, dt)
                at += n
            return t
        assert 2 * (6 * DW + 8 * ROWS + ROWS * AW) <= NG * FLAT
        d1 = [dense_tiles(runs, h) for h in range(2)]
        d2 = [dense_tiles(rows_flat, h) for h in range(2)]
        turned_sum = [part(joined, h * 512, [512]) for h in range(2)]

        turned_a = psum("turned_a", [P, W2], F32)
        turned_b = psum("turned_b", [P, W2], F32)
        ps_small = psum("ps_small", [P, 512], F32)
        ps_t = [turned_a[:, 0:512], turned_a[:, 512:1024]]
        ps_y = [turned_b[:, 0:512], turned_b[:, 512:1024]]

        s_edges = sem("edges_loaded")
        s_iota = sem("iotas_written")
        s_pooled = sem("pool_steps")
        s_dve = sem("dve_step_done")
        s_quads = sem("quad_records_built")
        s_recd = sem("quad_records_stored")
        s_tabini = sem("first_table_rows_written")
        s_mapd = sem("map_initialised")
        s_aggd = sem("sums_initialised")
        s_xcopy = sem("x_copied_to_tables")
        s_toturn = sem("sort_tiles_to_turn")
        s_turned = sem("sort_tiles_turned")
        s_sorted = sem("keys_sorted")
        s_keysd = sem("keys_stored")
        s_keys = sem("keys_loaded")
        s_wsel = sem("weights_selected")
        s_sqrt = sem("weights_rooted")
        s_ask = sem("small_turn_wanted")
        s_ans = sem("small_turn_done")
        s_idx = sem("indices_ready")
        s_land = [sem("even_stage_landed"), sem("odd_stage_landed")]
        s_rows = sem("rows_updated")
        s_rowsd = sem("rows_stored")
        s_gate = sem("pool_gate_passed")
        s_go1 = sem("layer0_rows_all_landed")
        s_go2 = sem("layer1_sums_all_landed")
        s_weights = sem("weights_loaded")
        s_in = [[sem(f"pass{k}_{h}_loaded") for h in range(2)] for k in range(2)]
        s_res = [sem(f"pass{k}_result_ready") for k in range(2)]
        s_resd = [[sem(f"pass{k}_{h}_stored") for h in range(2)] for k in range(2)]
        s_var = [sem(f"pass{k}_variance_ready") for k in range(2)]
        s_std = [sem(f"pass{k}_deviation_ready") for k in range(2)]
        s_pegate = sem("pe_gate_passed")
        s_settled = sem("dve_wait_ended")
        s_scaled = sem("sums_scaled")
        s_sumt = sem("sums_turned")
        s_sumc = sem("turned_sums_copied")
        s_mm = sem("products_ready")
        s_mmfree = sem("products_read")

        block = ctx.enter_context(nc.Block())

        PASSES = ["rec_a", "rec_b", "map_put", "map_get", "first"] + ["round"] * ITERATIONS + [
            "final_put", "attr", "x1_get", "agg_put"]
        FIRST = {}
        for k, name in enumerate(PASSES):
            FIRST.setdefault(name, k * NG)
        LANDED = 16 * GC
        PAIRS = NG // 2

        table_slots = [t[N:N + SLOTS, :].rearrange("(p c) f -> p c f", p=P) for t in table_d]

        def run_column(g, w):
            return runs[:, (g + 1) * FLAT:(g + 2) * FLAT].rearrange("p (f w) -> p f w", w=WIN)[:, :, w]

        @block.sync
        def _(sp):
            sp.dma_start(raw_edges[0:ER, 0, :], src.rearrange("(p c) -> p c", p=ER)).then_inc(s_edges, 16)
            sp.dma_start(raw_edges[0:ER, 1, :], dst.rearrange("(p c) -> p c", p=ER)).then_inc(s_edges, 16)
            sp.dma_start(raw_w[0:ER], edge_weight.rearrange("(p c) -> p c", p=ER)).then_inc(s_edges, 16)
            sp.wait_ge(s_tabini, 1)
            sp.dma_start(map_d.rearrange("(p r) f -> p (r f)", p=ER),
                         map_rows[0:ER].rearrange("p a b -> p (a b)")).then_inc(s_mapd, 16)
            sp.wait_ge(s_tabini, 2)
            pieces = N // (AP0 * AR)
            sp.dma_start(agg_d.rearrange("(p k r) f -> p k (r f)", p=AP0, k=pieces),
                         agg_rows[0:AP0].rearrange("p a b -> p (a b)").unsqueeze(1)
                         .to_broadcast([AP0, pieces, AR * AW])).then_inc(s_aggd, 16)
            sp.wait_ge(s_quads, 1)
            sp.dma_start(rec_d.rearrange("(p c) f -> p (c f)", p=ER),
                         rec[0:ER].rearrange("p a b c -> p (a b c)")).then_inc(s_recd, 16)
            sp.wait_ge(s_sorted, 1)
            sp.dma_start(keys_d[:, 0:LEAD], zero_i[:]).then_inc(s_keysd, 16)
            for a in range(2):
                sp.dma_start(keys_d[a, LEAD:LEAD + SORTED].rearrange("(p c) -> p c", p=P),
                             sort_buf[0][:, a * SIDE:(a + 1) * SIDE].bitcast(I32)).then_inc(s_keysd, 16)
            sp.wait_ge(s_keysd, 48)
            for a in range(2):
                around = bass.AP(keys_d.tensor, a * (LEAD + SORTED), [[COLS, P], [1, KW]])
                sp.dma_start(keys[:, a, :], around).then_inc(s_keys, 16)

            with sp.Fori(0, NG) as g:
                sp.wait_ge(s_rows, g + 1)
                sp.dma_start(table_slots[0][:, bass.ds(g * GC, GC), :],
                             rows[:, bass.ds(g, 1)].rearrange("p o c f -> p (o c) f")).then_inc(s_rowsd, 16)
            with sp.Fori(0, ITERATIONS // 2) as it:
                for half in range(2):
                    with sp.Fori(0, NG) as g:
                        sp.wait_ge(s_rows, it * (2 * NG) + g + (1 + NG * (half + 1)))
                        sp.dma_start(table_slots[1 - half][:, bass.ds(g * GC, GC), :],
                                     rows[:, bass.ds(g, 1)].rearrange("p o c f -> p (o c) f")).then_inc(s_rowsd, 16)

            def load_block(k, h, np_, lo):
                t = (d1, d2)[k][h]
                def flat(d, w):
                    return d[bass.ds(lo, np_ * ROWS), :].rearrange("(p r) f -> p (r f)", r=ROWS)
                def tile(name):
                    return t[name][0:np_].rearrange("p a b -> p (a b)")
                if k == 0:
                    sp.dma_start(tile("x"), flat(x, C)).then_inc(s_in[k][h], 16)
                    sp.dma_start(tile("f"), flat(table_d[0], C)).then_inc(s_in[k][h], 16)
                    sp.dma_start(tile("map"), flat(map_d, 2)).then_inc(s_in[k][h], 16)
                else:
                    sp.dma_start(tile("x"), flat(x1_d, C)).then_inc(s_in[k][h], 16)
                    sp.dma_start(tile("agg"), flat(agg_d, AW)).then_inc(s_in[k][h], 16)

            for k, per_block in ((0, 32), (1, 16)):
                sp.wait_ge((s_go1, s_go2)[k], 1)
                for h in range(2):
                    load_block(k, h, P, h * BLOCK)
                with sp.Fori(1, NB // 2) as i:
                    for h in range(2):
                        sp.wait_ge(s_resd[k][h], i * per_block)
                        load_block(k, h, P, i * (2 * BLOCK) + h * BLOCK)
                sp.wait_ge(s_resd[k][0], (NB // 2) * per_block)
                load_block(k, 0, TAILP, NB * BLOCK)
            sp.wait_ge(s_resd[1][0], (NB // 2 + 1) * 16)
            sp.wait_ge(s_resd[1][1], (NB // 2) * 16)

        @block.gpsimd
        def _(pool):
            nc.gpsimd.iota(sort_buf[0].bitcast(I32).rearrange("p (a c) -> p a c", a=2)[:, :, 0:EC],
                           [[0, 2], [1, EC]], base=N + KEY_OFFSET + P * (SIDE - EC) - ER * EC,
                           channel_multiplier=EC).then_inc(s_iota, 1)
            nc.gpsimd.iota(sort_buf[0].bitcast(I32).rearrange("p (a c) -> p a c", a=2)[:, :, EC:SIDE],
                           [[0, 2], [1, SIDE - EC]], base=N + KEY_OFFSET,
                           channel_multiplier=SIDE - EC).then_inc(s_iota, 1)
            nc.gpsimd.iota(quarter, [[1, EC // QUAD], [0, QUAD]], base=0,
                           channel_multiplier=EC // QUAD).then_inc(s_iota, 1)
            nc.gpsimd.iota(slot_i[:], [[1, COLS]], base=0, channel_multiplier=COLS).then_inc(s_iota, 1)
            nc.gpsimd.iota(small_i[:, 0:1], [[0, 1]], base=0, channel_multiplier=1).then_inc(s_iota, 1)
            nc.gpsimd.memset(ident[:], 0.0).then_inc(s_pooled, 1)
            pool.wait_ge(s_pooled, 1)
            nc.gpsimd.affine_select(out=ident[:], in_=ident[:], compare_op=ALU.not_equal, fill=1.0, base=0,
                                    pattern=[[-1, P]], channel_multiplier=1).then_inc(s_iota, 1)
            nc.gpsimd.memset(map_rows[0:ER, :, 1], 1).then_inc(s_pooled, 1)
            nc.gpsimd.iota(map_rows[0:ER, :, 0], [[1, MR]], base=0, channel_multiplier=MR).then_inc(s_pooled, 1)
            pool.wait_ge(s_pooled, 3)
            pool.sem_inc(s_tabini, 1)
            nc.gpsimd.memset(agg_rows[0:AP0, :, 0:C], 0.0).then_inc(s_pooled, 1)
            nc.gpsimd.memset(agg_rows[0:AP0, :, C:AW], 1.0).then_inc(s_pooled, 1)
            pool.wait_ge(s_pooled, 5)
            pool.sem_inc(s_tabini, 1)

            def rounds(width, table, first, dt=F32, put=False, limit=None):
                with pool.Fori(0, PAIRS) as i:
                    for h in range(2):
                        pool.wait_ge(s_idx, i * 2 + first + h + 1)
                        pool.sem_inc(s_gate, 1)
                        for c in range(GC):
                            piece = stage[:, h, c * width:(c + 1) * width]
                            if dt is not F32:
                                piece = piece.bitcast(dt)
                            at = bass.IndirectOffsetOnAxis(ap=stage_i[:, h, c:c + 1], axis=0)
                            if put:
                                nc.gpsimd.indirect_dma_start(table, at, piece, None, bounds_check=N - 1,
                                                             oob_is_err=False).then_inc(s_land[h], 16)
                            else:
                                nc.gpsimd.indirect_dma_start(piece, None, table, at).then_inc(s_land[h], 16)

            pool.wait_ge(s_recd, 16)
            rounds(3 * QUAD, rec_d, FIRST["rec_a"], I32)
            rounds(3 * QUAD, rec_d, FIRST["rec_b"], I32)
            pool.wait_ge(s_mapd, 16)
            rounds(2, map_d, FIRST["map_put"], I32, put=True)
            for h in range(2):
                pool.wait_ge(s_land[h], (FIRST["map_get"] // 2) * LANDED)
            rounds(2, map_d, FIRST["map_get"], I32)
            rounds(C, x, FIRST["first"])
            pool.wait_ge(s_xcopy, 32)
            with pool.Fori(0, ITERATIONS // 2) as it:
                for half in range(2):
                    pool.wait_ge(s_rowsd, it * (2 * NG * 16) + NG * 16 * (half + 1))
                    pool.sem_inc(s_gate, 1)
                    with pool.Fori(0, PAIRS) as i:
                        for h in range(2):
                            pool.wait_ge(s_idx, it * (2 * NG) + i * 2 + (FIRST["round"] + half * NG + h + 1))
                            pool.sem_inc(s_gate, 1)
                            for c in range(GC):
                                nc.gpsimd.indirect_dma_start(
                                    stage[:, h, c * C:(c + 1) * C], None, table_d[half],
                                    bass.IndirectOffsetOnAxis(ap=stage_i[:, h, c:c + 1], axis=0)
                                ).then_inc(s_land[h], 16)
            rounds(C, table_d[0], FIRST["final_put"], put=True)
            rounds(C, edge_attr, FIRST["attr"])
            for h in range(2):
                pool.wait_ge(s_resd[0][h], 32 * (NB // 2 + (1 if h == 0 else 0)))
            rounds(C, x1s_d, FIRST["x1_get"])
            pool.wait_ge(s_aggd, 16)
            rounds(AW, agg_d, FIRST["agg_put"], put=True)

        @block.scalar
        def _(act):
            for t in range(2):
                act.dma_start(table_d[t][0:N, :].rearrange("(p r) f -> p (r f)", p=800),
                              x.rearrange("(p r) f -> p (r f)", p=800)).then_inc(s_xcopy, 16)
            act.wait_ge(s_wsel, 1)
            nc.scalar.activation(wgt[:], wgt[:], ACT.Sqrt).then_inc(s_sqrt, 1)
            for k in range(QUAD):
                act.dma_start(wblk[k * C:(k + 1) * C, k * C:(k + 1) * C], weight).then_inc(s_weights, 16)
            act.dma_start(bias_b[:], bias.rearrange("(o f) -> o f", o=1).to_broadcast([P, C])).then_inc(s_weights, 16)

            def deviation(k, h, np_, n):
                t = (d1, d2)[k][h]
                act.wait_ge(s_var[k], n)
                nc.scalar.activation(t["std"][0:np_], t["var"][0:np_], ACT.Sqrt, scale=1.0 / C,
                                     bias=small[0:np_, 0:1]).then_inc(s_std[k], 1)

            def degree(k, h, np_, n):
                t = (d1, d2)[k][h]
                act.wait_ge(s_var[k], n)
                nc.scalar.activation(t["deg"][0:np_], t["deg"][0:np_], ACT.Sqrt).then_inc(s_std[k], 1)

            def store(k, h, np_, lo, n):
                t = (d1, d2)[k][h]
                def flat(d):
                    return d[bass.ds(lo, np_ * ROWS), :].rearrange("(p r) f -> p (r f)", r=ROWS)
                act.wait_ge(s_res[k], n)
                act.dma_start(flat((x1_d, out)[k]), t["o"][0:np_].rearrange("p a b -> p (a b)")).then_inc(s_resd[k][h], 16)
                if k == 0:
                    act.dma_start(flat(x1s_d), t["o2"][0:np_].rearrange("p a b -> p (a b)")).then_inc(s_resd[k][h], 16)

            def turned_copy(h, np_, n):
                act.wait_ge(s_sumt, n)
                nc.scalar.activation(turned_sum[h].rearrange("p (k n) -> p k n", k=QUAD)[:, :, 0:np_],
                                     ps_t[h].rearrange("p (k n) -> p k n", k=QUAD)[:, :, 0:np_],
                                     ACT.Copy).then_inc(s_sumc, 1)

            def blocks(k, i, np_, hs, base):
                for h in hs:
                    degree(k, h, np_, base * 2 + (h + 1) if len(hs) == 2 else base * 2 + 1)
                for h in hs:
                    if k == 1:
                        turned_copy(h, np_, base + (h + 1))
                for h in hs:
                    deviation(k, h, np_, base * 2 + (len(hs) + h + 1))
                for h in hs:
                    store(k, h, np_, base * BLOCK + h * BLOCK, base + (h + 1))

            for k in range(2):
                with act.Fori(0, NB // 2) as i:
                    blocks(k, i, P, (0, 1), i * 2)
                blocks(k, NB // 2, TAILP, (0,), NB)

        @block.tensor
        def _(pe):
            pe.wait_ge(s_iota, 6)
            for r in range(7):
                for back in range(2):
                    source = turn_buf[(r + 1) % 2] if back else sort_buf[0]
                    target = turned_b if back else turned_a
                    pe.wait_ge(s_toturn, 2 * r + back + 1)
                    for b in range(W2 // P):
                        t = nc.tensor.transpose(target[:, b * P:(b + 1) * P], source[:, b * P:(b + 1) * P], ident[:])
                    t.then_inc(s_turned, 1)
            asked = Count(s_ask)

            def small_turn(out_, in_, wait=True):
                n_in = in_.shape[0]
                if wait:
                    asked.n += 1
                    pe.wait_ge(s_ask, asked.value())
                    pe.sem_inc(s_pegate, 1)
                return nc.tensor.transpose(out_, in_, ident[0:n_in, 0:n_in])

            for a in range(2):
                t = small_turn(ps_small[0:1, a * P:(a + 1) * P], small[:, 8 + a:9 + a], wait=a == 0)
            t.then_inc(s_ans, 1)
            for a in range(2):
                t = small_turn(ps_small[:, 2 * P + a:2 * P + a + 1], line[0:1, a, 0:P], wait=a == 0)
            t.then_inc(s_ans, 1)
            small_turn(ps_small[0:1, 0:P], small[:, 10:11]).then_inc(s_ans, 1)
            for m in range(3):
                t = small_turn(ps_small[0:C, m * P:(m + 1) * P], cross_col[:, m, :], wait=m == 0)
            t.then_inc(s_ans, 1)

            def carries(g, x_, w):
                small_turn(ps_small[0:C, 0:P], run_column(g, x_)).then_inc(s_ans, 1)
                small_turn(ps_small[:, 2 * P:2 * P + C], ends_t[:, w, w:w + P]).then_inc(s_ans, 1)

            with pe.Fori(0, ITERATIONS) as it:
                start = asked.enter(it, 4)
                carries(NG - 1, GC, 0)
                carries(0, 1, 1)
                asked.leave(start, ITERATIONS)
            carries(NG - 1, GC, 0)

            def products(h, np_, n):
                t = d2[h]
                pe.wait_ge(s_scaled, n[1])
                for q in range(ROWS // QUAD):
                    tr = nc.tensor.transpose(ps_t[h][:, q * P:q * P + np_],
                                             t["f"][0:np_, q * QUAD:(q + 1) * QUAD].rearrange("p a b -> p (a b)"),
                                             ident[0:np_, 0:np_])
                tr.then_inc(s_sumt, 1)

            def multiply(h, np_, n):
                pe.wait_ge(s_sumc, n)
                pe.wait_ge(s_mmfree, n)
                for q in range(ROWS // QUAD):
                    mm = nc.tensor.matmul(ps_y[h][0:np_, q * P:(q + 1) * P], turned_sum[h][:, q * P:q * P + np_],
                                          wblk[:], start=True, stop=True)
                mm.then_inc(s_mm, 1)
            pe.wait_ge(s_weights, 80)
            with pe.Fori(0, NB // 2) as i:
                for h in range(2):
                    products(h, P, (i, i * 2 + (h + 1)))
                for h in range(2):
                    multiply(h, P, i * 2 + (h + 1))
            products(0, TAILP, (NB // 2, NB + 1))
            multiply(0, TAILP, NB + 1)

        @block.vector
        def _(v):
            V = nc.vector
            done = Count(s_dve)

            def settle():
                v.sem_inc(s_settled, 1)

            def step(instruction):
                done.inc(instruction)
                v.wait_ge(s_dve, done.value())

            step(V.memset(small[:, 0:1], EPS))
            step(V.memset(zero_i[:], 0))
            step(V.memset(ends_t[:], 0.0))
            step(V.memset(line[:], 0.0))
            step(V.memset(wblk[:], 0.0))
            for r in range(QUAD):
                step(V.memset(four[:, r:r + 1], float(r)))
            step(V.memset(match[:], 0.0))
            v.sem_inc(s_mmfree, 2)
            v.wait_ge(s_edges, 48)
            v.wait_ge(s_iota, 5)
            for a in range(2):
                step(V.tensor_copy(rec[0:ER, :, a, :], raw_edges[0:ER, a, :].rearrange("p (c q) -> p c q", q=QUAD)))
            step(V.tensor_copy(rec[0:ER, :, 2, :], raw_w[0:ER].bitcast(I32).rearrange("p (c q) -> p c q", q=QUAD)))
            v.sem_inc(s_quads, 1)
            key_i = sort_buf[0].bitcast(I32)
            key_e = key_i.rearrange("p (a c) -> p a c", a=2)[0:ER, :, 0:EC]
            step(V.tensor_scalar(key_e, raw_edges[0:ER], KEY_OFFSET, None, ALU.add))
            step(V.tensor_scalar(key_i, key_i, KEY_SHIFT, None, ALU.logical_shift_left))
            step(V.tensor_tensor(key_e, key_e, quarter[0:ER].unsqueeze(1).to_broadcast([ER, 2, EC]), ALU.bitwise_or))

            for b in range(7):
                step(V.tensor_scalar(small_i[:, 1:2], small_i[:, 0:1], b, None, ALU.logical_shift_right))
                step(V.tensor_scalar(small_i[:, 1:2], small_i[:, 1:2], 1, None, ALU.bitwise_and))
                step(V.tensor_scalar(small[:, 16 + b:17 + b], small_i[:, 1:2], -2.0, 1.0, ALU.mult, ALU.add))
            step(V.tensor_tensor(small[:, 24:30], small[:, 16:22], small[:, 17:23], ALU.mult))

            def compare(target, source, bit):
                s = source.rearrange("p (a h b) -> p a h b", h=2, b=1 << bit)
                t = target.rearrange("p (a h b) -> p a h b", h=2, b=1 << bit)
                done.inc(V.tensor_tensor(t[:, :, 0, :], s[:, :, 0, :], s[:, :, 1, :], ALU.min))
                step(V.tensor_tensor(t[:, :, 1, :], s[:, :, 0, :], s[:, :, 1, :], ALU.max))

            def flip(buf, bit):
                s = buf.rearrange("p (a h b) -> p a h b", h=2, b=1 << bit)
                step(V.tensor_scalar(s[:, :, 1, :], s[:, :, 1, :], -1.0, None, ALU.mult))

            SIDE_BITS = 9
            at = 0
            for k in range(1, SIDE_BITS + 1):
                if k < SIDE_BITS:
                    flip(sort_buf[at], k)
                else:
                    step(V.tensor_scalar(sort_buf[at], sort_buf[at], small[:, 16:17], None, ALU.mult))
                for j in reversed(range(k)):
                    compare(sort_buf[1 - at], sort_buf[at], j)
                    at = 1 - at
                if k < SIDE_BITS:
                    flip(sort_buf[at], k)
            for r in range(7):
                sign = small[:, 24 + r:25 + r] if r < 6 else small[:, 22:23]
                step(V.tensor_scalar(sort_buf[0], sort_buf[at], sign, None, ALU.mult))
                v.sem_inc(s_toturn, 1)
                v.wait_ge(s_turned, 2 * r + 1)
                step(V.tensor_copy(turn_buf[0], turned_a[:]))
                turn = 0
                for j in reversed(range(r + 1)):
                    compare(turn_buf[1 - turn], turn_buf[turn], j)
                    turn = 1 - turn
                v.sem_inc(s_toturn, 1)
                v.wait_ge(s_turned, 2 * r + 2)
                step(V.tensor_copy(sort_buf[1], turned_b[:]))
                at = 1
                for j in reversed(range(SIDE_BITS)):
                    compare(sort_buf[1 - at], sort_buf[at], j)
                    at = 1 - at
            v.sem_inc(s_sorted, 1)

            v.wait_ge(s_keys, 32)
            own = slice(LEAD, LEAD + COLS)
            node_i = part(window, 0, [2 * KW], I32).rearrange("p (a c) -> p a c", a=2)
            step(V.tensor_scalar(node_i, keys[:], KEY_SHIFT, None, ALU.logical_shift_right))
            step(V.tensor_scalar(node[:], node_i, -KEY_OFFSET, None, ALU.add))
            step(V.tensor_scalar(quad[:], keys[:, :, own], (1 << KEY_SHIFT) - 1, None, ALU.bitwise_and))
            keyf = keys[:].bitcast(F32)

            def before(t, d):
                return t[:, :, LEAD - d:LEAD - d + COLS]

            step(V.tensor_tensor(twin[:], keyf[:, :, own], before(keyf, 1), ALU.is_equal))
            for d in (2, 3):
                step(V.tensor_tensor(same[:], keyf[:, :, own], before(keyf, d), ALU.is_equal))
                step(V.tensor_tensor(twin[:], twin[:], same[:], ALU.add))
            step(V.tensor_tensor(same[:], node[:, :, own], before(node, 1), ALU.is_equal))
            slot_f = diff[:].rearrange("p c f -> p (c f)")[:, 0:COLS]
            head = diff[:].rearrange("p c f -> p (c f)")[:, COLS:2 * COLS]
            step(V.tensor_copy(slot_f, slot_i[:]))
            for a in range(2):
                step(V.tensor_scalar(head, same[:, a], -1.0, 1.0, ALU.mult, ALU.add))
                step(V.tensor_tensor(head, head, slot_f, ALU.mult))
                step(v.tensor_tensor_scan(length[:, a], head, head, 0.0, ALU.max, ALU.max))
                step(V.tensor_copy(small[:, 8 + a:9 + a], length[:, a, COLS - 1:COLS]))
            asks = Count(s_ask)
            answers = Count(s_ans)

            def ask():
                asks.n += 1
                v.sem_inc(s_ask, 1)
                answers.n += 1
                v.wait_ge(s_ans, answers.value())

            ask()
            for a in range(2):
                step(V.tensor_copy(line[0:1, 2 + a, 0:P], ps_small[0:1, a * P:(a + 1) * P]))
                step(v.tensor_tensor_scan(line[0:1, a, 1:P + 1], line[0:1, 2 + a, 0:P], line[0:1, 2 + a, 0:P], 0.0,
                                          ALU.max, ALU.max))
            ask()
            step(V.tensor_copy(small[:, 8:10], ps_small[:, 2 * P:2 * P + 2]))
            for a in range(2):
                step(V.tensor_scalar(length[:, a], length[:, a], small[:, 8 + a:9 + a], None, ALU.max))
                step(V.tensor_tensor(length[:, a], slot_f, length[:, a], ALU.subtract))
            step(V.tensor_scalar(length[:], length[:], 1.0, None, ALU.add))
            step(V.tensor_reduce(small[:, 10:11], length[:].rearrange("p a c -> p (a c)"), AX.X, ALU.max))
            ask()
            step(V.tensor_reduce(longest[:], ps_small[0:1, 0:P], AX.X, ALU.max))
            lastf = part(window, 0, [2 * COLS]).rearrange("p (a c) -> p a c", a=2)
            step(V.tensor_tensor(lastf, node[:, :, own], node[:, :, LEAD + 1:LEAD + 1 + COLS], ALU.is_equal))
            step(V.scalar_tensor_tensor(last_i[:], lastf, float(1 << 20), node[:, :, own], ALU.mult, ALU.add))
            step(V.tensor_scalar(clip[:], node[:, 0, own], float(N - 1), None, ALU.min))
            step(V.memset(cross[:], 0.0))
            for m, (a, at_, scale) in enumerate(((0, LEAD - 1, BIG), (0, LEAD + COLS, BIG), (1, LEAD - 1, 1.0))):
                step(V.tensor_scalar(cross[:, m, 1:], node[:, a, own], node[:, a, at_:at_ + 1], scale,
                                     ALU.is_equal, ALU.mult))
                far = 1 if m == 1 else COLS
                step(V.tensor_copy(cross_col[:, m, :], cross[:, m, far:far + 1].to_broadcast([P, C])))
            ask()
            step(V.tensor_copy(whole[:].rearrange("c m p -> c (m p)"), ps_small[0:C, 0:3 * P]))
            long_runs = v.value_load(longest[0:1, 0:1], min_val=0, max_val=SLOTS) > NEAR

            def window_of(tile, g):
                return tile[:, bass.ds(g * FLAT, FLAT)].rearrange("p (f w) -> p f w", w=WIN)

            def build_masks(a, scale):
                settle()
                with v.Fori(0, NG) as g:
                    start = done.enter(g, 1)
                    step(V.tensor_scalar(window_of(joined, g)[:, :, 1:],
                                         same[:, a, bass.ds(g * GC, GC)].unsqueeze(1).to_broadcast([P, C, GC]),
                                         scale, None, ALU.mult))
                    settle()
                    done.leave(start, NG)

            step(V.memset(joined[:], 0.0))
            build_masks(0, BIG)
            step(V.memset(runs[:, 0:FLAT], 0.0))

            def one_pass(first, fill, consume, steps, fills, outer=None):
                def landed(i, h):
                    r = i * LANDED + (first // 2 + 1) * LANDED
                    if outer is not None:
                        r = outer * (NG * LANDED) + r
                    v.wait_ge(s_land[h], r)

                def filled(g, h):
                    fill(g, h)
                    v.sem_inc(s_idx, 1)

                for h in range(2):
                    filled(h, h)
                settle()
                with v.Fori(0, PAIRS - 1) as i:
                    start = done.enter(i, 2 * (steps + fills))
                    for h in range(2):
                        landed(i, h)
                        consume(i * 2 + h, h)
                        filled(i * 2 + (h + 2), h)
                    settle()
                    done.leave(start, PAIRS - 1)
                for h in range(2):
                    landed(PAIRS - 1, h)
                    consume(NG - 2 + h, h)

            def group(tile, g):
                return tile[..., bass.ds(g * GC, GC)]

            def put_indices(tile, g, h):
                step(V.tensor_scalar(stage_i[:, h, :], tile[:, bass.ds(g * GC, GC)], 0, None, ALU.add))

            def select(a, wanted, twice):
                def consume(g, h):
                    rec4 = stage[:, h, 0:GC * 3 * QUAD].bitcast(I32).rearrange("p (c k q) -> p c k q", k=3, q=QUAD)
                    m, cnt, sel, prod = (match[:, k] for k in range(4))
                    step(V.tensor_tensor(m, rec4[:, :, a, :], node[:, a, bass.ds(g * GC + LEAD, GC)].unsqueeze(2)
                                         .to_broadcast([P, GC, QUAD]), ALU.is_equal))
                    step(V.tensor_scalar(cnt[:, :, 1:2], m[:, :, 0:1], 1.0, None, ALU.mult))
                    step(V.tensor_tensor(cnt[:, :, 2:3], cnt[:, :, 1:2], m[:, :, 1:2], ALU.add))
                    step(V.tensor_tensor(cnt[:, :, 3:4], cnt[:, :, 2:3], m[:, :, 2:3], ALU.add))
                    step(V.tensor_tensor(sel, cnt, twin[:, a, bass.ds(g * GC, GC)].unsqueeze(2)
                                         .to_broadcast([P, GC, QUAD]), ALU.is_equal))
                    step(V.tensor_tensor(sel, sel, m, ALU.mult))
                    for values, target in wanted(rec4, g):
                        step(V.tensor_tensor(prod, sel, values, ALU.mult))
                        step(V.tensor_tensor(prod[:, :, 0:2], prod[:, :, 0:2], prod[:, :, 2:4], ALU.add))
                        step(V.tensor_tensor(target, prod[:, :, 0:1], prod[:, :, 1:2], ALU.add))
                return consume

            def of_a(rec4, g):
                return ((rec4[:, :, 1, :], other[:, 0, bass.ds(g * GC, GC)].unsqueeze(2)),
                        (rec4[:, :, 2, :].bitcast(F32), wgt[:, bass.ds(g * GC, GC)].unsqueeze(2)))

            def of_b(rec4, g):
                return ((rec4[:, :, 0, :], other[:, 1, bass.ds(g * GC, GC)].unsqueeze(2)),
                        (four[:].unsqueeze(1).to_broadcast([P, GC, QUAD]),
                         edge_b[:, bass.ds(g * GC, GC)].unsqueeze(2)))

            one_pass(FIRST["rec_a"], lambda g, h: put_indices(quad[:, 0], g, h), select(0, of_a, 2), 12, 1)
            v.sem_inc(s_wsel, 1)
            one_pass(FIRST["rec_b"], lambda g, h: put_indices(quad[:, 1], g, h), select(1, of_b, 2), 12, 1)
            step(V.scalar_tensor_tensor(edge_b[:], quad[:, 1], float(QUAD), edge_b[:], ALU.mult, ALU.add))

            def fill_map(g, h):
                pair = stage[:, h, 0:2 * GC].bitcast(I32).rearrange("p (c k) -> p c k", k=2)
                step(V.tensor_scalar(pair[:, :, 0], slot_i[:, bass.ds(g * GC, GC)], N, None, ALU.add))
                step(V.tensor_scalar(pair[:, :, 1], length[:, 0, bass.ds(g * GC, GC)], 1.0, None, ALU.mult))
                put_indices(last_i[:, 0], g, h)

            one_pass(FIRST["map_put"], fill_map, lambda g, h: None, 0, 3)

            def take_map(g, h):
                pair = stage[:, h, 0:2 * GC].bitcast(I32).rearrange("p (c k) -> p c k", k=2)
                step(V.tensor_scalar(gidx[:, bass.ds(g * GC, GC)], pair[:, :, 0], 0, None, ALU.add))

            one_pass(FIRST["map_get"], lambda g, h: put_indices(other[:, 0], g, h), take_map, 1, 1)

            def stage_rows(h):
                return stage[:, h, 0:GC * C].rearrange("p (c f) -> p c f", f=C)

            def rows_of(g):
                return rows[:, bass.ds(g, 1)].rearrange("p o c f -> p (o c) f")

            def take_rows(g, h):
                step(V.tensor_scalar(rows_of(g), stage_rows(h), 1.0, None, ALU.mult))
                v.sem_inc(s_rows, 1)

            v.wait_ge(s_mapd, 16)
            v.wait_ge(s_aggd, 16)
            one_pass(FIRST["first"], lambda g, h: put_indices(clip, g, h), take_rows, 1, 1)

            win = window[:].rearrange("p (f w) -> p f w", w=WIN)

            def carry_in(g):
                step(V.tensor_scalar(win[:, :, 0:1],
                                     runs[:, bass.ds(g * FLAT, FLAT)].rearrange("p (f w) -> p f w", w=WIN)[:, :, GC:WIN],
                                     1.0, None, ALU.mult))

            def scan_forward(g, op0, op1):
                step(v.tensor_tensor_scan(runs[:, bass.ds(g * FLAT + FLAT, FLAT)], joined[:, bass.ds(g * FLAT, FLAT)],
                                          window[:], 0.0, op0, op1))

            def rises(g, h):
                step(V.tensor_tensor(diff[:], stage_rows(h), rows_of(g), ALU.subtract))
                carry_in(g)
                step(V.scalar_tensor_tensor(win[:, :, 1:].rearrange("p f c -> p c f"), diff[:], 0.0,
                                            wgt[:, bass.ds(g * GC, GC)].unsqueeze(2).to_broadcast([P, GC, C]),
                                            ALU.max, ALU.mult))
                scan_forward(g, ALU.min, ALU.max)

            def run_win(g):
                return runs[:, bass.ds(g * FLAT + FLAT, FLAT)].rearrange("p (f w) -> p f w", w=WIN)

            def apply(g, m, w0, w1, op0, op1):
                n = w1 - w0
                step(V.tensor_tensor(fix[:, :, 0:n],
                                     cross[:, m, bass.ds(g * GC + w0, n)].unsqueeze(1).to_broadcast([P, C, n]),
                                     ps_small[:, 2 * P:2 * P + C].unsqueeze(2).to_broadcast([P, C, n]), op0))
                step(V.tensor_tensor(run_win(g)[:, :, w0:w1], run_win(g)[:, :, w0:w1], fix[:, :, 0:n], op1))

            def over_partitions(m, backward, op0, op1):
                ask()
                if backward:
                    step(v.tensor_tensor_scan(ends_t[:, 1, 0:P][:, ::-1],
                                              whole[:, m, ::-1], ps_small[0:C, 0:P][:, ::-1], 0.0, op0, op1))
                else:
                    step(v.tensor_tensor_scan(ends_t[:, 0, 1:P + 1], whole[:, m, :], ps_small[0:C, 0:P], 0.0, op0, op1))
                ask()
                if backward:
                    near, far = (NG - 1, WIN - NEAR, WIN), (NG - 1, 1, WIN - NEAR)
                    rest, w0 = (0, NG - 1), 1
                else:
                    near, far = (0, 1, 1 + NEAR), (0, 1 + NEAR, WIN)
                    rest, w0 = (1, NG), 0
                apply(near[0], m, near[1], near[2], op0, op1)
                before_if = done.n
                far_steps = 2 + 2 * (rest[1] - rest[0])
                settle()
                with v.If(long_runs):
                    apply(far[0], m, far[1], far[2], op0, op1)
                    settle()
                    with v.Fori(0, rest[1] - rest[0]) as g:
                        start = done.enter(g, 2)
                        apply(g + rest[0], m, w0, WIN, op0, op1)
                        settle()
                        done.leave(start, rest[1] - rest[0])
                with v.Else():
                    v.sem_inc(s_dve, far_steps)
                assert done.n - before_if == far_steps
                v.wait_ge(s_dve, done.value())

            def scan_backward(g):
                at = (g + 1) * FLAT
                step(v.tensor_tensor_scan(runs[:, at:at + FLAT][:, ::-1], joined[:, g * FLAT + 1:(g + 1) * FLAT + 1][:, ::-1],
                                          runs[:, at:at + FLAT][:, ::-1], 0.0, ALU.min, ALU.max))

            v.wait_ge(s_sqrt, 1)
            settle()
            with v.Fori(0, ITERATIONS // 2) as it:
                per = 2 * (NG * 5 + (3 + 2 * NG) + (3 + 2 * NG) + (1 + 2 * (NG - 1)) + NG)
                start = done.enter(it, per)
                astart, bstart = asks.enter(it, 8), answers.enter(it, 8)
                for half in range(2):
                    one_pass(FIRST["round"] + half * NG, lambda g, h: put_indices(gidx, g, h), rises, 4, 1, outer=it)
                    over_partitions(0, False, ALU.min, ALU.max)
                    scan_backward(NG - 1)
                    for g in reversed(range(NG - 1)):
                        step(V.tensor_scalar(run_win(g)[:, :, GC:WIN], run_win(g + 1)[:, :, 0:1], 1.0, None, ALU.mult))
                        scan_backward(g)
                    over_partitions(1, True, ALU.min, ALU.max)
                    settle()
                    with v.Fori(0, NG) as g:
                        inner = done.enter(g, 1)
                        step(V.tensor_tensor(rows_of(g), rows_of(g), run_win(g)[:, :, 1:].rearrange("p f c -> p c f"), ALU.add))
                        v.sem_inc(s_rows, 1)
                        settle()
                        done.leave(inner, NG)
                settle()
                done.leave(start, ITERATIONS // 2)
                asks.leave(astart, ITERATIONS // 2)
                answers.leave(bstart, ITERATIONS // 2)

            def fill_rows(g, h):
                step(V.tensor_scalar(stage_rows(h), rows_of(g), 1.0, None, ALU.mult))
                put_indices(last_i[:, 0], g, h)

            one_pass(FIRST["final_put"], fill_rows, lambda g, h: None, 0, 2)
            v.sem_inc(s_go1, 1)
            v.wait_ge(s_rowsd, 16 * NG * (ITERATIONS + 1))
            def take_attr(g, h):
                step(V.tensor_scalar(rows_of(g), stage_rows(h), 1.0, None, ALU.mult))
            one_pass(FIRST["attr"], lambda g, h: put_indices(edge_b, g, h), take_attr, 1, 1)

            def each(hs, f):
                for h in hs:
                    f(h)

            def dense(k, np_, hs, i, first):
                t = (d1, d2)[k]
                def bc(a):
                    return a[0:np_].unsqueeze(2).to_broadcast([np_, ROWS, C])
                def residual(h):
                    u = t[h]
                    v.wait_ge(s_in[k][h], (i + 1) * (48 if k == 0 else 32))
                    if k == 0:
                        step(V.tensor_copy(u["deg"][0:np_], u["map"][0:np_, :, 1]))
                        v.sem_inc(s_var[k], 1)
                        step(V.tensor_tensor(u["y"][0:np_], u["x"][0:np_], u["f"][0:np_], ALU.add))
                    else:
                        step(V.tensor_copy(u["deg"][0:np_], u["agg"][0:np_, :, C]))
                        v.sem_inc(s_var[k], 1)
                def scale(h):
                    u = t[h]
                    if k == 1:
                        v.wait_ge(s_std[k], first * 2 + (h + 1))
                        step(V.reciprocal(u["mean"][0:np_], u["deg"][0:np_]))
                        step(V.tensor_tensor(u["f"][0:np_], u["agg"][0:np_, :, 0:C], bc(u["mean"]), ALU.mult))
                        v.sem_inc(s_scaled, 1)
                def product(h):
                    u = t[h]
                    if k == 1:
                        v.wait_ge(s_mm, first + (h + 1))
                        step(V.tensor_tensor(u["y"][0:np_], ps_y[h][0:np_].rearrange("p (r f) -> p r f", f=C),
                                             bias_b[0:np_].unsqueeze(1).to_broadcast([np_, ROWS, C]), ALU.add))
                        v.sem_inc(s_mmfree, 1)
                        step(V.tensor_tensor(u["y"][0:np_], u["y"][0:np_], u["x"][0:np_], ALU.add))
                def centre(h):
                    u = t[h]
                    step(V.tensor_reduce(u["sum"][0:np_], u["y"][0:np_], AX.X, ALU.add))
                    step(V.tensor_scalar(u["mean"][0:np_], u["sum"][0:np_], 1.0 / C, None, ALU.mult))
                    step(V.tensor_tensor(u["y"][0:np_], u["y"][0:np_], bc(u["mean"]), ALU.subtract))
                    step(V.tensor_tensor(u["sq"][0:np_], u["y"][0:np_], u["y"][0:np_], ALU.mult))
                    step(V.tensor_reduce(u["var"][0:np_], u["sq"][0:np_], AX.X, ALU.add))
                    v.sem_inc(s_var[k], 1)
                def norm(h):
                    u = t[h]
                    v.wait_ge(s_std[k], first * 2 + (len(hs) + h + 1))
                    step(V.reciprocal(u["rstd"][0:np_], u["std"][0:np_]))
                    step(V.tensor_tensor(u["o"][0:np_], u["y"][0:np_], bc(u["rstd"]), ALU.mult))
                    if k == 0:
                        step(V.reciprocal(u["mean"][0:np_], u["deg"][0:np_]))
                        step(V.tensor_tensor(u["o2"][0:np_], u["o"][0:np_], bc(u["mean"]), ALU.mult))
                    v.sem_inc(s_res[k], 1)
                for stage_ in (residual, scale, product, centre, norm):
                    each(hs, stage_)
                return

            def dense_pass(k):
                per = 2 * ((2 + 5 + 4) if k == 0 else (1 + 4 + 5 + 2))
                settle()
                with v.Fori(0, NB // 2) as i:
                    start = done.enter(i, per)
                    dense(k, P, (0, 1), i, i * 2)
                    settle()
                    done.leave(start, NB // 2)
                dense(k, TAILP, (0,), NB // 2, NB)

            dense_pass(0)

            step(V.memset(joined[:], 0.0))
            build_masks(1, 1.0)
            for h in range(2):
                v.wait_ge(s_resd[0][h], 32 * (NB // 2 + (1 if h == 0 else 0)))
            step(V.memset(runs[:, 0:FLAT], 0.0))

            def messages(g, h):
                carry_in(g)
                step(V.tensor_tensor(win[:, :, 1:].rearrange("p f c -> p c f"), stage_rows(h), rows_of(g), ALU.add))
                scan_forward(g, ALU.mult, ALU.add)

            one_pass(FIRST["x1_get"], lambda g, h: put_indices(other[:, 1], g, h), messages, 3, 1)
            over_partitions(2, False, ALU.mult, ALU.add)

            def fill_sums(g, h):
                target = stage[:, h, :].rearrange("p (c f) -> p c f", f=AW)
                step(V.tensor_scalar(target[:, :, 0:C], run_win(g)[:, :, 1:].rearrange("p f c -> p c f"), 1.0, None, ALU.mult))
                step(V.tensor_scalar(target[:, :, C:AW], length[:, 1, bass.ds(g * GC, GC)].unsqueeze(2), 1.0, None, ALU.mult))
                put_indices(last_i[:, 1], g, h)

            one_pass(FIRST["agg_put"], fill_sums, lambda g, h: None, 0, 3)
            v.sem_inc(s_go2, 1)
            dense_pass(1)


_INS = ["x", "src", "dst", "edge_attr_32", "edge_weight", "L1_gnn_weight", "L1_gnn_bias"]


def kernel(**inputs):
    import numpy as _np
    import concourse.bacc as _bacc
    from concourse import mybir as _mybir
    from concourse.bass_utils import run_bass_kernel_spmd as _run

    nc = _bacc.Bacc("TRN2", target_bir_lowering=False, num_devices=1)
    arrays, args = {}, []
    for name in _INS:
        a = _np.ascontiguousarray(inputs[name])
        arrays[f"in_{name}_dram"] = a
        args.append(nc.dram_tensor(f"in_{name}_dram", a.shape, _mybir.dt.from_np(a.dtype), kind="ExternalInput").ap())
    shape = arrays["in_x_dram"].shape
    args.append(nc.dram_tensor("out_0_dram", shape, _mybir.dt.float32, kind="ExternalOutput").ap())
    resnorm_gnn(nc, *args)
    r = _run(nc, [arrays], core_ids=[0])
    return r.results[0]["out_0_dram"]
```

```python
from contextlib import ExitStack

import concourse.bass as bass
from concourse import mybir

ALU = mybir.AluOpType
ACT = mybir.ActivationFunctionType
AX = mybir.AxisListType
F32 = mybir.dt.float32
I32 = mybir.dt.int32

P = 128
GC = 28
QUAD = 4
BIG = 3.0e38
KEY_SHIFT = 14
KEY_OFFSET = 512
ITERATIONS = 10
EPS = 1e-5
NEAR = 8
ROWS = 16


class Count:

    def __init__(self, sem, step=1):
        self.sem, self.step, self.n, self.loops = sem, step, 0, []

    def inc(self, instruction):
        self.n += 1
        return instruction.then_inc(self.sem, self.step)

    def value(self):
        v = self.n * self.step
        for i, per in self.loops:
            v = i * (per * self.step) + v
        return v

    def enter(self, i, per):
        self.loops.append((i, per))
        return self.n

    def leave(self, start, trips):
        _, per = self.loops.pop()
        assert self.n - start == per, (self.n - start, per)
        self.n = start + per * trips


def resnorm_gnn(nc, x, src, dst, edge_attr, edge_weight, weight, bias, out, debug=None):
    N, C = x.shape
    E = src.shape[0]
    SIDE = 512
    COLS = -(-E // (P * 2 * GC)) * 2 * GC
    NG = COLS // GC
    SLOTS = P * COLS
    SORTED = P * SIDE
    ER = 100
    EC = E // ER
    LEAD = 16
    KW = LEAD + COLS + LEAD
    WIN = GC + 1
    FLAT = C * WIN
    assert E == ER * EC and EC % QUAD == 0 and EC <= SIDE and NG % 2 == 0 and SLOTS <= SORTED
    assert N + KEY_OFFSET + (SORTED - E) < 1 << 17 and E // QUAD < 1 << KEY_SHIFT
    BLOCK = P * ROWS
    NB = N // BLOCK
    TAILP = (N - NB * BLOCK) // ROWS
    assert NB % 2 == 0 and NB * BLOCK + TAILP * ROWS == N
    AW = C + 1

    def scratch(name, shape, dt):
        kind = "ExternalOutput" if debug and name in debug else "Internal"
        return nc.dram_tensor(name, shape, dt, kind=kind).ap()

    keys_d = scratch("keys_d", [2, LEAD + SORTED], I32)
    rec_d = scratch("rec_d", [E // QUAD, 3 * QUAD], I32)
    map_d = scratch("map_d", [N, 1], I32)
    table_d = [scratch("table0_d", [N + SLOTS, C], F32), scratch("table1_d", [N + SLOTS, C], F32)]
    first_d = scratch("first_d", [SLOTS, C], F32)
    x1_d = scratch("x1_d", [N, AW], F32)
    dst_d = scratch("dst_d", [SLOTS], I32)
    src_d = scratch("src_d", [SLOTS], I32)
    attr_d = scratch("attr_d", [SLOTS, C], F32)
    agg_d = scratch("agg_d", [N, AW], F32)

    with ExitStack() as ctx:
        def sb(name, shape, dt):
            return ctx.enter_context(nc.sbuf_tensor(name, shape, dt))

        def psum(name, shape, dt):
            return ctx.enter_context(nc.psum_tensor(name, shape, dt))

        def sem(name):
            return ctx.enter_context(nc.semaphore(name))

        runs = sb("runs", [P, (NG + 1) * FLAT], F32)
        joined = sb("joined", [P, NG * FLAT + 1], F32)
        rows = sb("rows", [P, NG, GC, C], F32)
        stage = sb("stage", [P, 2, GC * AW], F32)
        stage_i = sb("stage_i", [P, 2, GC], I32)
        window = sb("window", [P, FLAT], F32)
        diff = sb("diff", [P, GC, C], F32)
        node = sb("node", [P, 2, KW], F32)
        other = sb("other", [P, 2, COLS], I32)
        edge_b = sb("edge_b", [P, COLS], I32)
        wgt = sb("wgt", [P, COLS], F32)
        gidx = sb("gidx", [P, COLS + 2 * GC], I32)
        tbuf = sb("tbuf", [P, 2, GC, C], F32)
        near_rows = sb("near_rows", [P, NEAR, C], F32)
        stats = sb("stats", [P, 5, GC], F32)
        degree_root = sb("degree_root", [P, COLS], F32)
        last_i = sb("last_i", [P, 2, COLS], I32)
        length = sb("length", [P, 2, COLS], F32)
        slot_i = sb("slot_i", [P, COLS], I32)
        ident = sb("ident", [P, P], F32)
        small = sb("small", [P, 64], F32)
        small_i = sb("small_i", [P, 8], I32)
        four = sb("four", [P, QUAD], F32)
        cross = sb("cross", [P, 3, 1 + COLS], F32)
        cross_col = sb("cross_col", [P, 3, C], F32)
        whole = sb("whole", [C, 3, P], F32)
        ends_t = sb("ends_t", [C, 2, P + 1], F32)
        flags = sb("flags", [1, 2], I32)
        pads = sb("pads", [2, SLOTS - E], I32)
        zero_i = sb("zero_i", [2, LEAD], I32)
        wblk = sb("wblk", [P, P], F32)
        bias_b = sb("bias_b", [P, C], F32)

        AP0Z = 88
        assert (SLOTS - E) * C % AP0Z == 0
        def part(tile, start, shape, dt=F32):
            size = 1
            for n in shape:
                size *= n
            v = tile[:, start:start + size]
            if dt is not F32:
                v = v.bitcast(dt)
            if len(shape) == 2:
                v = v.rearrange("p (a b) -> p a b", a=shape[0])
            if len(shape) == 3:
                v = v.rearrange("p (a b c) -> p a b c", a=shape[0], b=shape[1])
            return v

        W2 = 2 * SIDE
        sort_buf = [runs[:, 0:W2], runs[:, W2:2 * W2]]
        turn_buf = [runs[:, 2 * W2:3 * W2], runs[:, 3 * W2:4 * W2]]
        raw_edges = part(runs, 4 * W2, [2, EC], I32)
        raw_w = part(runs, 4 * W2 + 2 * EC, [EC])
        quarter = part(runs, 4 * W2 + 3 * EC, [EC], I32)
        rec = part(runs, 4 * W2 + 4 * EC, [EC // QUAD, 3, QUAD], I32)
        TEMP = 4 * W2 + 7 * EC
        same = part(runs, TEMP, [2, COLS])
        match = part(runs, TEMP + 2 * COLS, [4 * GC * QUAD]).rearrange("p (k c q) -> p k c q", k=4, q=QUAD)
        dst_slots = part(runs, TEMP + 2 * COLS + 4 * GC * QUAD, [COLS], I32)
        line = part(runs, TEMP + 3 * COLS + 4 * GC * QUAD, [4, P + 1])[0:1]
        assert TEMP + 3 * COLS + 4 * GC * QUAD + 4 * (P + 1) <= NG * FLAT
        zeros = part(joined, 0, [(SLOTS - E) * C // AP0Z])
        rows_flat = rows[:].rearrange("p g c f -> p (g c f)")
        MR = N // ER
        map_rows = part(rows_flat, 0, [MR], I32)
        AP0, AR = 80, 25
        agg_rows = part(rows_flat, MR, [AR, AW])
        KA = 2 * MR + AR * AW
        keys = part(rows_flat, KA, [2, KW], I32)
        quad = part(rows_flat, KA + 2 * KW, [2, COLS], I32)
        twin = part(rows_flat, KA + 2 * KW + 2 * COLS, [2, COLS])
        assert KA + 2 * KW + 4 * COLS <= NG * GC * C and N % (AP0 * AR) == 0 and N % ER == 0

        fix = window[:].rearrange("p (f w) -> p f w", w=WIN)

        DW = ROWS * C
        DENSE = 3 * DW + 6 * ROWS + 3 * ROWS * AW

        def dense_tiles(tile, h):
            at = h * DENSE
            t = {}
            for name, shape in (("x", [ROWS, AW]), ("agg", [ROWS, AW]), ("o", [ROWS, AW]), ("f", [ROWS, C]),
                                ("y", [ROWS, C]), ("sq", [ROWS, C]), ("sum", [ROWS]), ("mean", [ROWS]),
                                ("var", [ROWS]), ("std", [ROWS]), ("rstd", [ROWS]), ("deg", [ROWS])):
                n = shape[0] * (shape[1] if len(shape) > 1 else 1)
                t[name] = part(tile, at, shape)
                at += n
            return t
        assert 2 * DENSE <= NG * FLAT
        d1 = [dense_tiles(runs, h) for h in range(2)]
        d2 = [dense_tiles(rows_flat, h) for h in range(2)]
        turned_sum = [part(joined, h * 512, [512]) for h in range(2)]

        turned_a = psum("turned_a", [P, W2], F32)
        turned_b = psum("turned_b", [P, W2], F32)
        ps_small = psum("ps_small", [P, 512], F32)
        ps_t = [turned_a[:, 0:512], turned_a[:, 512:1024]]
        ps_y = [turned_b[:, 0:512], turned_b[:, 512:1024]]

        s_edges = sem("edges_loaded")
        s_iota = sem("iotas_written")
        s_pooled = sem("pool_steps")
        s_dve = sem("dve_step_done")
        s_quads = sem("quad_records_built")
        s_recd = sem("quad_records_stored")
        s_tabini = sem("first_table_rows_written")
        s_mapd = sem("map_initialised")
        s_aggd = sem("sums_initialised")
        s_xcopy = sem("x_copied_to_tables")
        s_padded = sem("inputs_padded")
        s_padt = sem("pad_tiles_written")
        s_dsts = sem("dst_slots_loaded")
        s_flags = sem("flags_written")
        s_toturn = sem("sort_tiles_to_turn")
        s_turned = sem("sort_tiles_turned")
        s_sorted = sem("keys_sorted")
        s_keysd = sem("keys_stored")
        s_keys = sem("keys_loaded")
        s_wsel = sem("weights_selected")
        s_sqrt = sem("weights_rooted")
        s_ask = sem("small_turn_wanted")
        s_ans = sem("small_turn_done")
        s_idx = sem("indices_ready")
        s_land = [sem("even_stage_landed"), sem("odd_stage_landed")]
        s_rows = sem("rows_updated")
        s_firstd = sem("first_rows_stored")
        s_table = sem("table_rows_ready")
        s_tabled = [sem("even_table_rows_stored"), sem("odd_table_rows_stored")]
        s_near = sem("near_rows_ready")
        s_neard = sem("near_rows_stored")
        s_again = sem("long_run_rows_ready")
        s_againd = sem("long_run_rows_stored")
        s_xfree = sem("norm_buffer_free")
        s_xin = [sem("even_norm_rows_loaded"), sem("odd_norm_rows_loaded")]
        s_nvar = sem("norm_variance_ready")
        s_nstd = sem("norm_deviation_ready")
        s_deg = sem("out_degrees_ready")
        s_degroot = sem("out_degrees_rooted")
        s_gate = sem("pool_gate_passed")
        s_go1 = sem("block_buffers_usable")
        s_go2 = sem("layer1_sums_all_landed")
        s_weights = sem("weights_loaded")
        s_in = [[sem(f"pass{k}_{h}_loaded") for h in range(2)] for k in range(2)]
        s_res = [sem(f"pass{k}_result_ready") for k in range(2)]
        s_resd = [[sem(f"pass{k}_{h}_stored") for h in range(2)] for k in range(2)]
        s_var = [sem(f"pass{k}_variance_ready") for k in range(2)]
        s_std = [sem(f"pass{k}_deviation_ready") for k in range(2)]
        s_pegate = sem("pe_gate_passed")
        s_settled = sem("dve_wait_ended")
        s_scaled = sem("sums_scaled")
        s_sumt = sem("sums_turned")
        s_sumc = sem("turned_sums_copied")
        s_mm = sem("products_ready")
        s_mmfree = sem("products_read")

        block = ctx.enter_context(nc.Block())

        PASSES = ["rec_a", "rec_b", "map_put", "map_get", "first"] + ["round"] * ITERATIONS + [
            "final_put", "attr", "x1_get", "agg_put"]
        FIRST = {}
        for k, name in enumerate(PASSES):
            FIRST.setdefault(name, k * NG)
        LANDED = 16 * GC
        PAIRS = NG // 2

        IDX_AHEAD = 2
        table_slots = [t[N:N + SLOTS, :].rearrange("(p c) f -> p c f", p=P) for t in table_d]

        def run_column(g, w):
            return runs[:, (g + 1) * FLAT:(g + 2) * FLAT].rearrange("p (f w) -> p f w", w=WIN)[:, :, w]

        @block.sync
        def _(sp):
            sp.dma_start(raw_edges[0:ER, 0, :], src.rearrange("(p c) -> p c", p=ER)).then_inc(s_edges, 16)
            sp.dma_start(raw_edges[0:ER, 1, :], dst.rearrange("(p c) -> p c", p=ER)).then_inc(s_edges, 16)
            sp.dma_start(raw_w[0:ER], edge_weight.rearrange("(p c) -> p c", p=ER)).then_inc(s_edges, 16)
            sp.wait_ge(s_tabini, 1)
            sp.dma_start(map_d.rearrange("(p r) f -> p (r f)", p=ER), map_rows[0:ER]).then_inc(s_mapd, 16)
            sp.wait_ge(s_tabini, 2)
            pieces = N // (AP0 * AR)
            sp.dma_start(agg_d.rearrange("(p k r) f -> p k (r f)", p=AP0, k=pieces),
                         agg_rows[0:AP0].rearrange("p a b -> p (a b)").unsqueeze(1)
                         .to_broadcast([AP0, pieces, AR * AW])).then_inc(s_aggd, 16)
            sp.wait_ge(s_quads, 1)
            sp.dma_start(rec_d.rearrange("(p c) f -> p (c f)", p=ER),
                         rec[0:ER].rearrange("p a b c -> p (a b c)")).then_inc(s_recd, 16)
            sp.wait_ge(s_sorted, 1)
            sp.dma_start(keys_d[:, 0:LEAD], zero_i[:]).then_inc(s_keysd, 16)
            for a in range(2):
                sp.dma_start(keys_d[a, LEAD:LEAD + SORTED].rearrange("(p c) -> p c", p=P),
                             sort_buf[0][:, a * SIDE:(a + 1) * SIDE].bitcast(I32)).then_inc(s_keysd, 16)
            sp.wait_ge(s_keysd, 48)
            for a in range(2):
                around = bass.AP(keys_d.tensor, a * (LEAD + SORTED), [[COLS, P], [1, KW]])
                sp.dma_start(keys[:, a, :], around).then_inc(s_keys, 16)
            sp.wait_ge(s_padded, 96)
            sp.dma_start(dst_slots, dst_d.rearrange("(p c) -> p c", p=P)).then_inc(s_dsts, 16)

            def group_rows(g):
                return rows[:, bass.ds(g, 1)].rearrange("p o c f -> p (o c) f")

            kept = first_d.rearrange("(p c) f -> p c f", p=P)
            with sp.Fori(0, PAIRS) as i:
                for h in range(2):
                    g = i * 2 + h
                    sp.wait_ge(s_rows, g + 1)
                    sp.dma_start(table_slots[0][:, bass.ds(g * GC, GC), :], group_rows(g)).then_inc(s_tabled[h], 16)
                    sp.dma_start(kept[:, bass.ds(g * GC, GC), :], group_rows(g)).then_inc(s_firstd, 16)
            sp.wait_ge(s_tabled[0], PAIRS * 16)
            sp.dma_start(table_slots[0][:, 0:NEAR, :], rows[:, 0, 0:NEAR, :]).then_inc(s_neard, 16)
            long_runs = sp.value_load(flags[0:1, 0:1], min_val=0, max_val=SLOTS) > NEAR
            with sp.Fori(0, ITERATIONS // 2) as it:
                for half in range(2):
                    table = table_slots[1 - half]
                    with sp.Fori(0, PAIRS) as i:
                        for h in range(2):
                            sp.wait_ge(s_table, it * (2 * NG) + i * 2 + (half * NG + h + 1))
                            sp.dma_start(table[:, bass.ds((i * 2 + h) * GC, GC), :], tbuf[:, h]).then_inc(s_tabled[h], 16)
                    with sp.If(long_runs):
                        with sp.Fori(0, NG) as g:
                            sp.wait_ge(s_again, it * (2 * NG) + g + (half * NG + 1))
                            sp.dma_start(table[:, bass.ds(g * GC, GC), :], tbuf[:, 0]).then_inc(s_againd, 16)
                    sp.wait_ge(s_near, it * 2 + (half + 1))
                    sp.dma_start(table[:, 0:NEAR, :], near_rows[:]).then_inc(s_neard, 16)

            with sp.Fori(0, PAIRS) as i:
                for h in range(2):
                    sp.wait_ge(s_xfree, i * 2 + h + 1)
                    sp.dma_start(tbuf[:, h], kept[:, bass.ds((i * 2 + h) * GC, GC), :]).then_inc(s_xin[h], 16)

            def load_block(h, np_, lo):
                for name, table in (("x", x1_d), ("agg", agg_d)):
                    sp.dma_start(d2[h][name][0:np_].rearrange("p a b -> p (a b)"),
                                 table[bass.ds(lo, np_ * ROWS), :].rearrange("(p r) f -> p (r f)", r=ROWS)
                                 ).then_inc(s_in[1][h], 16)

            sp.wait_ge(s_go2, 1)
            for h in range(2):
                load_block(h, P, h * BLOCK)
            with sp.Fori(1, NB // 2) as i:
                for h in range(2):
                    sp.wait_ge(s_resd[1][h], i * 16)
                    load_block(h, P, i * (2 * BLOCK) + h * BLOCK)
            sp.wait_ge(s_resd[1][0], (NB // 2) * 16)
            load_block(0, TAILP, NB * BLOCK)
            sp.wait_ge(s_resd[1][0], (NB // 2 + 1) * 16)
            sp.wait_ge(s_resd[1][1], (NB // 2) * 16)

        @block.gpsimd
        def _(pool):
            nc.gpsimd.iota(sort_buf[0].bitcast(I32).rearrange("p (a c) -> p a c", a=2)[:, :, 0:EC],
                           [[0, 2], [1, EC]], base=N + KEY_OFFSET + P * (SIDE - EC) - ER * EC,
                           channel_multiplier=EC).then_inc(s_iota, 1)
            nc.gpsimd.iota(sort_buf[0].bitcast(I32).rearrange("p (a c) -> p a c", a=2)[:, :, EC:SIDE],
                           [[0, 2], [1, SIDE - EC]], base=N + KEY_OFFSET,
                           channel_multiplier=SIDE - EC).then_inc(s_iota, 1)
            nc.gpsimd.iota(quarter, [[1, EC // QUAD], [0, QUAD]], base=0,
                           channel_multiplier=EC // QUAD).then_inc(s_iota, 1)
            nc.gpsimd.iota(slot_i[:], [[1, COLS]], base=0, channel_multiplier=COLS).then_inc(s_iota, 1)
            nc.gpsimd.iota(small_i[:, 0:1], [[0, 1]], base=0, channel_multiplier=1).then_inc(s_iota, 1)
            nc.gpsimd.memset(ident[:], 0.0).then_inc(s_pooled, 1)
            pool.wait_ge(s_pooled, 1)
            nc.gpsimd.affine_select(out=ident[:], in_=ident[:], compare_op=ALU.not_equal, fill=1.0, base=0,
                                    pattern=[[-1, P]], channel_multiplier=1).then_inc(s_iota, 1)
            nc.gpsimd.iota(map_rows[0:ER], [[1, MR]], base=0, channel_multiplier=MR).then_inc(s_pooled, 1)
            pool.wait_ge(s_pooled, 2)
            pool.sem_inc(s_tabini, 1)
            nc.gpsimd.memset(agg_rows[0:AP0, :, 0:C], 0.0).then_inc(s_pooled, 1)
            nc.gpsimd.memset(agg_rows[0:AP0, :, C:AW], 1.0).then_inc(s_pooled, 1)
            pool.wait_ge(s_pooled, 4)
            pool.sem_inc(s_tabini, 1)

            def rounds(width, table, first, dt=F32, put=False, limit=None):
                with pool.Fori(0, PAIRS) as i:
                    for h in range(2):
                        pool.wait_ge(s_idx, i * 2 + first + h + 1)
                        pool.sem_inc(s_gate, 1)
                        for c in range(GC):
                            piece = stage[:, h, c * width:(c + 1) * width]
                            if dt is not F32:
                                piece = piece.bitcast(dt)
                            at = bass.IndirectOffsetOnAxis(ap=stage_i[:, h, c:c + 1], axis=0)
                            if put:
                                nc.gpsimd.indirect_dma_start(table, at, piece, None, bounds_check=N - 1,
                                                             oob_is_err=False).then_inc(s_land[h], 16)
                            else:
                                nc.gpsimd.indirect_dma_start(piece, None, table, at).then_inc(s_land[h], 16)

            def load_groups(target, source):
                with pool.Fori(0, PAIRS) as i:
                    for h in range(2):
                        for part_ in range(2):
                            cols = bass.ds((i * 2 + h) * GC + part_ * (GC // 2), GC // 2)
                            pool.dma_start(target[:, cols], source[:, cols]).then_inc(s_land[h], LANDED // 2)

            pool.wait_ge(s_recd, 16)
            rounds(3 * QUAD, rec_d, FIRST["rec_a"], I32)
            in_order = pool.value_load(flags[0:1, 1:2], min_val=0, max_val=1)
            with pool.If(in_order == 0):
                rounds(3 * QUAD, rec_d, FIRST["rec_b"], I32)
            with pool.Else():
                pool.wait_ge(s_idx, FIRST["rec_b"] + NG)
                pool.sem_inc(s_gate, 1)
                load_groups(other[:, 1], src_d.rearrange("(p c) -> p c", p=P))
            pool.wait_ge(s_mapd, 16)
            rounds(1, map_d, FIRST["map_put"], I32, put=True)
            for h in range(2):
                pool.wait_ge(s_land[h], (FIRST["map_get"] // 2) * LANDED)
            rounds(1, map_d, FIRST["map_get"], I32)
            rounds(C, x, FIRST["first"])
            pool.wait_ge(s_xcopy, 32)
            with pool.Fori(0, ITERATIONS // 2) as it:
                for half in range(2):
                    for h in range(2):
                        pool.wait_ge(s_tabled[h], it * (2 * PAIRS * 16) + PAIRS * 16 * (half + 1))
                    pool.wait_ge(s_neard, it * 32 + 16 * (half + 1))
                    pool.sem_inc(s_gate, 1)
                    with pool.Fori(0, PAIRS) as i:
                        for h in range(2):
                            pool.wait_ge(s_idx, it * (2 * NG) + i * 2 + (FIRST["round"] + half * NG + h + 1))
                            pool.sem_inc(s_gate, 1)
                            for c in range(GC):
                                nc.gpsimd.indirect_dma_start(
                                    stage[:, h, c * C:(c + 1) * C], None, table_d[half],
                                    bass.IndirectOffsetOnAxis(ap=stage_i[:, h, c:c + 1], axis=0)
                                ).then_inc(s_land[h], 16)
            for h in range(2):
                pool.wait_ge(s_resd[0][h], 16 * (NB // 2 + (1 if h == 0 else 0)))
            rounds(AW, x1_d, FIRST["final_put"] + IDX_AHEAD, put=True)
            with pool.If(in_order == 0):
                rounds(C, edge_attr, FIRST["attr"] + IDX_AHEAD)
            with pool.Else():
                pool.wait_ge(s_idx, FIRST["attr"] + NG + IDX_AHEAD)
                pool.sem_inc(s_gate, 1)
                load_groups(rows[:].rearrange("p g c f -> p (g c) f"), attr_d.rearrange("(p c) f -> p c f", p=P))
            for h in range(2):
                pool.wait_ge(s_land[h], (FIRST["attr"] // 2) * LANDED)
            rounds(AW, x1_d, FIRST["x1_get"] + IDX_AHEAD)
            pool.wait_ge(s_aggd, 16)
            rounds(AW, agg_d, FIRST["agg_put"] + IDX_AHEAD, put=True)

        @block.scalar
        def _(act):
            act.dma_start(dst_d[0:E].rearrange("(p c) -> p c", p=80), dst.rearrange("(p c) -> p c", p=80)).then_inc(s_padded, 16)
            act.dma_start(src_d[0:E].rearrange("(p c) -> p c", p=80), src.rearrange("(p c) -> p c", p=80)).then_inc(s_padded, 16)
            act.dma_start(attr_d[0:E, :].rearrange("(p r) f -> p (r f)", p=400),
                          edge_attr.rearrange("(p r) f -> p (r f)", p=400)).then_inc(s_padded, 16)
            act.wait_ge(s_padt, 1)
            for m, d in enumerate((dst_d, src_d)):
                act.dma_start(d[E:SLOTS].rearrange("(o c) -> o c", o=1), pads[m:m + 1, :]).then_inc(s_padded, 16)
            act.dma_start(attr_d[E:SLOTS, :].rearrange("(p r) f -> p (r f)", p=AP0Z), zeros[0:AP0Z]).then_inc(s_padded, 16)
            for t in range(2):
                act.dma_start(table_d[t][0:N, :].rearrange("(p r) f -> p (r f)", p=800),
                              x.rearrange("(p r) f -> p (r f)", p=800)).then_inc(s_xcopy, 16)
            act.wait_ge(s_deg, 1)
            nc.scalar.activation(degree_root[:], degree_root[:], ACT.Sqrt).then_inc(s_degroot, 1)
            for k in range(QUAD):
                act.dma_start(wblk[k * C:(k + 1) * C, k * C:(k + 1) * C], weight).then_inc(s_weights, 16)
            act.dma_start(bias_b[:], bias.rearrange("(o f) -> o f", o=1).to_broadcast([P, C])).then_inc(s_weights, 16)
            act.wait_ge(s_wsel, 1)
            nc.scalar.activation(wgt[:], wgt[:], ACT.Sqrt).then_inc(s_sqrt, 1)

            def root(k, h, np_, n):
                t = (d1, d2)[k][h]
                act.wait_ge(s_var[k], n)
                nc.scalar.activation(t["std"][0:np_], t["var"][0:np_], ACT.Sqrt, scale=1.0 / C,
                                     bias=small[0:np_, 0:1]).then_inc(s_std[k], 1)

            def degree(h, np_, n):
                act.wait_ge(s_var[1], n)
                nc.scalar.activation(d2[h]["deg"][0:np_], d2[h]["deg"][0:np_], ACT.Sqrt).then_inc(s_std[1], 1)

            def turned_copy(h, np_, n):
                act.wait_ge(s_sumt, n)
                nc.scalar.activation(turned_sum[h].rearrange("p (k n) -> p k n", k=QUAD)[:, :, 0:np_],
                                     ps_t[h].rearrange("p (k n) -> p k n", k=QUAD)[:, :, 0:np_],
                                     ACT.Copy).then_inc(s_sumc, 1)

            def store(k, h, np_, lo, n):
                t = (d1, d2)[k][h]
                act.wait_ge(s_res[k], n)
                if k == 0:
                    act.dma_start(x1_d[bass.ds(lo, np_ * ROWS), :].rearrange("(p r) f -> p (r f)", r=ROWS),
                                  t["o"][0:np_].rearrange("p a b -> p (a b)")).then_inc(s_resd[k][h], 16)
                else:
                    act.dma_start(out[bass.ds(lo, np_ * ROWS), :].rearrange("(p r) f -> p (r f)", r=ROWS),
                                  t["f"][0:np_].rearrange("p a b -> p (a b)")).then_inc(s_resd[k][h], 16)

            def load_x(h, np_, lo):
                act.dma_start(d1[h]["y"][0:np_].rearrange("p a b -> p (a b)"),
                              x[bass.ds(lo, np_ * ROWS), :].rearrange("(p r) f -> p (r f)", r=ROWS)
                              ).then_inc(s_in[0][h], 16)

            act.wait_ge(s_go1, 1)
            for h in range(2):
                load_x(h, P, h * BLOCK)
            with act.Fori(1, NB // 2) as i:
                for h in range(2):
                    root(0, h, P, i * 2 + (h - 1))
                for h in range(2):
                    store(0, h, P, (i - 1) * (2 * BLOCK) + h * BLOCK, i * 2 + (h - 1))
                for h in range(2):
                    act.wait_ge(s_resd[0][h], i * 16)
                    load_x(h, P, i * (2 * BLOCK) + h * BLOCK)
            for h in range(2):
                root(0, h, P, NB + h - 1)
            for h in range(2):
                store(0, h, P, (NB - 2 + h) * BLOCK, NB + h - 1)
            act.wait_ge(s_resd[0][0], (NB // 2) * 16)
            load_x(0, TAILP, NB * BLOCK)
            root(0, 0, TAILP, NB + 1)
            store(0, 0, TAILP, NB * BLOCK, NB + 1)

            with act.Fori(0, NG) as g:
                act.wait_ge(s_nvar, g + 1)
                nc.scalar.activation(stats[:, 3], stats[:, 2], ACT.Sqrt, scale=1.0 / C,
                                     bias=small[:, 0:1]).then_inc(s_nstd, 1)

            def blocks(np_, hs, base):
                for h in hs:
                    degree(h, np_, base * 2 + (h + 1))
                for h in hs:
                    turned_copy(h, np_, base + (h + 1))
                for h in hs:
                    root(1, h, np_, base * 2 + (len(hs) + h + 1))
                for h in hs:
                    store(1, h, np_, base * BLOCK + h * BLOCK, base + (h + 1))

            with act.Fori(0, NB // 2) as i:
                blocks(P, (0, 1), i * 2)
            blocks(TAILP, (0,), NB)

        @block.tensor
        def _(pe):
            pe.wait_ge(s_iota, 6)
            for r in range(7):
                for back in range(2):
                    source = turn_buf[(r + 1) % 2] if back else sort_buf[0]
                    target = turned_b if back else turned_a
                    pe.wait_ge(s_toturn, 2 * r + back + 1)
                    for b in range(W2 // P):
                        t = nc.tensor.transpose(target[:, b * P:(b + 1) * P], source[:, b * P:(b + 1) * P], ident[:])
                    t.then_inc(s_turned, 1)
            asked = Count(s_ask)

            def small_turn(out_, in_, wait=True):
                n_in = in_.shape[0]
                if wait:
                    asked.n += 1
                    pe.wait_ge(s_ask, asked.value())
                    pe.sem_inc(s_pegate, 1)
                return nc.tensor.transpose(out_, in_, ident[0:n_in, 0:n_in])

            for a in range(2):
                t = small_turn(ps_small[0:1, a * P:(a + 1) * P], small[:, 8 + a:9 + a], wait=a == 0)
            t.then_inc(s_ans, 1)
            for a in range(2):
                t = small_turn(ps_small[:, 2 * P + a:2 * P + a + 1], line[0:1, a, 0:P], wait=a == 0)
            t.then_inc(s_ans, 1)
            for m in range(2):
                t = small_turn(ps_small[0:1, m * P:(m + 1) * P], small[:, 10 + m:11 + m], wait=m == 0)
            t.then_inc(s_ans, 1)
            for m in range(3):
                t = small_turn(ps_small[0:C, m * P:(m + 1) * P], cross_col[:, m, :], wait=m == 0)
            t.then_inc(s_ans, 1)

            def carries(g, x_, w):
                small_turn(ps_small[0:C, 0:P], run_column(g, x_)).then_inc(s_ans, 1)
                small_turn(ps_small[:, 2 * P:2 * P + C], ends_t[:, w, w:w + P]).then_inc(s_ans, 1)

            with pe.Fori(0, ITERATIONS) as it:
                start = asked.enter(it, 4)
                carries(NG - 1, GC, 0)
                carries(0, 1, 1)
                asked.leave(start, ITERATIONS)
            carries(NG - 1, GC, 0)

            def turn_sums(h, np_, n):
                t = d2[h]
                pe.wait_ge(s_scaled, n)
                for q in range(ROWS // QUAD):
                    tr = nc.tensor.transpose(ps_t[h][:, q * P:q * P + np_],
                                             t["f"][0:np_, q * QUAD:(q + 1) * QUAD].rearrange("p a b -> p (a b)"),
                                             ident[0:np_, 0:np_])
                tr.then_inc(s_sumt, 1)

            def multiply(h, np_, n):
                pe.wait_ge(s_sumc, n)
                pe.wait_ge(s_mmfree, n)
                for q in range(ROWS // QUAD):
                    mm = nc.tensor.matmul(ps_y[h][0:np_, q * P:(q + 1) * P], turned_sum[h][:, q * P:q * P + np_],
                                          wblk[:], start=True, stop=True)
                mm.then_inc(s_mm, 1)
            pe.wait_ge(s_weights, 80)
            with pe.Fori(0, NB // 2) as i:
                for h in range(2):
                    turn_sums(h, P, i * 2 + (h + 1))
                for h in range(2):
                    multiply(h, P, i * 2 + (h + 1))
            turn_sums(0, TAILP, NB + 1)
            multiply(0, TAILP, NB + 1)

        @block.vector
        def _(v):
            V = nc.vector
            done = Count(s_dve)

            def settle():
                v.sem_inc(s_settled, 1)

            def step(instruction):
                done.inc(instruction)
                v.wait_ge(s_dve, done.value())

            step(V.memset(small[:, 0:1], EPS))
            step(V.memset(zero_i[:], 0))
            step(V.memset(ends_t[:], 0.0))
            step(V.memset(line, 0.0))
            step(V.memset(wblk[:], 0.0))
            for r in range(QUAD):
                step(V.memset(four[:, r:r + 1], float(r)))
            step(V.memset(match[:], 0.0))
            v.sem_inc(s_mmfree, 2)
            step(V.memset(zeros, 0.0))
            step(V.memset(pads[:], 0))
            step(V.memset(pads[0:1, :], N))
            v.sem_inc(s_padt, 1)
            v.wait_ge(s_edges, 48)
            v.wait_ge(s_iota, 5)
            for a in range(2):
                step(V.tensor_copy(rec[0:ER, :, a, :], raw_edges[0:ER, a, :].rearrange("p (c q) -> p c q", q=QUAD)))
            step(V.tensor_copy(rec[0:ER, :, 2, :], raw_w[0:ER].bitcast(I32).rearrange("p (c q) -> p c q", q=QUAD)))
            v.sem_inc(s_quads, 1)
            key_i = sort_buf[0].bitcast(I32)
            key_e = key_i.rearrange("p (a c) -> p a c", a=2)[0:ER, :, 0:EC]
            step(V.tensor_scalar(key_e, raw_edges[0:ER], KEY_OFFSET, None, ALU.add))
            step(V.tensor_scalar(key_i, key_i, KEY_SHIFT, None, ALU.logical_shift_left))
            step(V.tensor_tensor(key_e, key_e, quarter[0:ER].unsqueeze(1).to_broadcast([ER, 2, EC]), ALU.bitwise_or))

            for b in range(7):
                step(V.tensor_scalar(small_i[:, 1:2], small_i[:, 0:1], b, None, ALU.logical_shift_right))
                step(V.tensor_scalar(small_i[:, 1:2], small_i[:, 1:2], 1, None, ALU.bitwise_and))
                step(V.tensor_scalar(small[:, 16 + b:17 + b], small_i[:, 1:2], -2.0, 1.0, ALU.mult, ALU.add))
            step(V.tensor_tensor(small[:, 24:30], small[:, 16:22], small[:, 17:23], ALU.mult))

            def compare(target, source, bit):
                s = source.rearrange("p (a h b) -> p a h b", h=2, b=1 << bit)
                t = target.rearrange("p (a h b) -> p a h b", h=2, b=1 << bit)
                done.inc(V.tensor_tensor(t[:, :, 0, :], s[:, :, 0, :], s[:, :, 1, :], ALU.min))
                step(V.tensor_tensor(t[:, :, 1, :], s[:, :, 0, :], s[:, :, 1, :], ALU.max))

            def flip(buf, bit):
                s = buf.rearrange("p (a h b) -> p a h b", h=2, b=1 << bit)
                step(V.tensor_scalar(s[:, :, 1, :], s[:, :, 1, :], -1.0, None, ALU.mult))

            SIDE_BITS = 9
            at = 0
            for k in range(1, SIDE_BITS + 1):
                if k < SIDE_BITS:
                    flip(sort_buf[at], k)
                else:
                    step(V.tensor_scalar(sort_buf[at], sort_buf[at], small[:, 16:17], None, ALU.mult))
                for j in reversed(range(k)):
                    compare(sort_buf[1 - at], sort_buf[at], j)
                    at = 1 - at
                if k < SIDE_BITS:
                    flip(sort_buf[at], k)
            for r in range(7):
                sign = small[:, 24 + r:25 + r] if r < 6 else small[:, 22:23]
                step(V.tensor_scalar(sort_buf[0], sort_buf[at], sign, None, ALU.mult))
                v.sem_inc(s_toturn, 1)
                v.wait_ge(s_turned, 2 * r + 1)
                step(V.tensor_copy(turn_buf[0], turned_a[:]))
                turn = 0
                for j in reversed(range(r + 1)):
                    compare(turn_buf[1 - turn], turn_buf[turn], j)
                    turn = 1 - turn
                v.sem_inc(s_toturn, 1)
                v.wait_ge(s_turned, 2 * r + 2)
                step(V.tensor_copy(sort_buf[1], turned_b[:]))
                at = 1
                for j in reversed(range(SIDE_BITS)):
                    compare(sort_buf[1 - at], sort_buf[at], j)
                    at = 1 - at
            v.sem_inc(s_sorted, 1)

            v.wait_ge(s_keys, 32)
            own = slice(LEAD, LEAD + COLS)
            node_i = part(window, 0, [2 * KW], I32).rearrange("p (a c) -> p a c", a=2)
            step(V.tensor_scalar(node_i, keys[:], KEY_SHIFT, None, ALU.logical_shift_right))
            step(V.tensor_scalar(node[:], node_i, -KEY_OFFSET, None, ALU.add))
            step(V.tensor_scalar(quad[:], keys[:, :, own], (1 << KEY_SHIFT) - 1, None, ALU.bitwise_and))
            keyf = keys[:].bitcast(F32)

            def before(t, d):
                return t[:, :, LEAD - d:LEAD - d + COLS]

            step(V.tensor_tensor(twin[:], keyf[:, :, own], before(keyf, 1), ALU.is_equal))
            for d in (2, 3):
                step(V.tensor_tensor(same[:], keyf[:, :, own], before(keyf, d), ALU.is_equal))
                step(V.tensor_tensor(twin[:], twin[:], same[:], ALU.add))
            step(V.tensor_tensor(same[:], node[:, :, own], before(node, 1), ALU.is_equal))
            slot_f = diff[:].rearrange("p c f -> p (c f)")[:, 0:COLS]
            head = diff[:].rearrange("p c f -> p (c f)")[:, COLS:2 * COLS]
            step(V.tensor_copy(slot_f, slot_i[:]))
            for a in range(2):
                step(V.tensor_scalar(head, same[:, a], -1.0, 1.0, ALU.mult, ALU.add))
                step(V.tensor_tensor(head, head, slot_f, ALU.mult))
                step(v.tensor_tensor_scan(length[:, a], head, head, 0.0, ALU.max, ALU.max))
                step(V.tensor_copy(small[:, 8 + a:9 + a], length[:, a, COLS - 1:COLS]))
            asks = Count(s_ask)
            answers = Count(s_ans)

            def ask():
                asks.n += 1
                v.sem_inc(s_ask, 1)
                answers.n += 1
                v.wait_ge(s_ans, answers.value())

            ask()
            for a in range(2):
                step(V.tensor_copy(line[0:1, 2 + a, 0:P], ps_small[0:1, a * P:(a + 1) * P]))
                step(v.tensor_tensor_scan(line[0:1, a, 1:P + 1], line[0:1, 2 + a, 0:P], line[0:1, 2 + a, 0:P], 0.0,
                                          ALU.max, ALU.max))
            ask()
            step(V.tensor_copy(small[:, 8:10], ps_small[:, 2 * P:2 * P + 2]))
            for a in range(2):
                step(V.tensor_scalar(length[:, a], length[:, a], small[:, 8 + a:9 + a], None, ALU.max))
                step(V.tensor_tensor(length[:, a], slot_f, length[:, a], ALU.subtract))
            step(V.tensor_scalar(length[:], length[:], 1.0, None, ALU.add))
            step(V.tensor_reduce(small[:, 10:11], length[:].rearrange("p a c -> p (a c)"), AX.X, ALU.max))
            v.wait_ge(s_dsts, 16)
            step(V.tensor_scalar(same[:, 0], node[:, 1, own], float(N), None, ALU.min))
            step(V.tensor_tensor(same[:, 0], same[:, 0], dst_slots, ALU.is_equal))
            step(V.tensor_reduce(small[:, 11:12], same[:, 0], AX.X, ALU.min))
            ask()
            step(V.tensor_reduce(flags[:, 0:1], ps_small[0:1, 0:P], AX.X, ALU.max))
            step(V.tensor_reduce(flags[:, 1:2], ps_small[0:1, P:2 * P], AX.X, ALU.min))
            v.sem_inc(s_flags, 1)
            step(V.tensor_copy(degree_root[:], length[:, 0]))
            v.sem_inc(s_deg, 1)
            lastf = part(window, 0, [2 * COLS]).rearrange("p (a c) -> p a c", a=2)
            step(V.tensor_tensor(lastf, node[:, :, own], node[:, :, LEAD + 1:LEAD + 1 + COLS], ALU.is_equal))
            step(V.scalar_tensor_tensor(last_i[:], lastf, float(1 << 20), node[:, :, own], ALU.mult, ALU.add))
            step(V.memset(cross[:], 0.0))
            for m, (a, at_, scale) in enumerate(((0, LEAD - 1, BIG), (0, LEAD + COLS, BIG), (1, LEAD - 1, 1.0))):
                step(V.tensor_scalar(cross[:, m, 1:], node[:, a, own], node[:, a, at_:at_ + 1], scale,
                                     ALU.is_equal, ALU.mult))
                far = 1 if m == 1 else COLS
                step(V.tensor_copy(cross_col[:, m, :], cross[:, m, far:far + 1].to_broadcast([P, C])))
            ask()
            step(V.tensor_copy(whole[:].rearrange("c m p -> c (m p)"), ps_small[0:C, 0:3 * P]))
            long_runs = v.value_load(flags[0:1, 0:1], min_val=0, max_val=SLOTS) > NEAR
            in_order = v.value_load(flags[0:1, 1:2], min_val=0, max_val=1)
            v.wait_ge(s_degroot, 1)
            step(V.reciprocal(degree_root[:], degree_root[:]))

            def window_of(tile, g):
                return tile[:, bass.ds(g * FLAT, FLAT)].rearrange("p (f w) -> p f w", w=WIN)

            def build_masks(a, scale):
                settle()
                with v.Fori(0, NG) as g:
                    start = done.enter(g, 2)
                    step(V.tensor_tensor(stats[:, 0], node[:, a, bass.ds(g * GC + LEAD, GC)],
                                         node[:, a, bass.ds(g * GC + (LEAD - 1), GC)], ALU.is_equal))
                    step(V.tensor_scalar(window_of(joined, g)[:, :, 1:],
                                         stats[:, 0].unsqueeze(1).to_broadcast([P, C, GC]), scale, None, ALU.mult))
                    settle()
                    done.leave(start, NG)

            v.wait_ge(s_padded, 96)
            step(V.memset(joined[:], 0.0))
            build_masks(0, BIG)

            def one_pass(first, fill, consume, steps, fills, beside=None, beside_steps=0):
                for h in range(2):
                    fill(h, h, 0)
                    v.sem_inc(s_idx, 1)
                settle()
                with v.Fori(0, PAIRS - 1) as i:
                    start = done.enter(i, 2 * (steps + fills) + beside_steps)
                    for h in range(2):
                        v.wait_ge(s_land[h], i * LANDED + (first // 2 + 1) * LANDED)
                        consume(i * 2 + h, h)
                        fill(i * 2 + (h + 2), h, i + 1)
                        v.sem_inc(s_idx, 1)
                    if beside:
                        beside(i)
                    settle()
                    done.leave(start, PAIRS - 1)
                for h in range(2):
                    v.wait_ge(s_land[h], (first // 2 + PAIRS) * LANDED)
                    consume(NG - 2 + h, h)

            def otherwise(condition, general, else_, steps):
                before = done.n
                settle()
                with v.If(condition):
                    general()
                    settle()
                with v.Else():
                    else_()
                    v.sem_inc(s_dve, steps)
                assert done.n - before == steps, (done.n - before, steps)
                v.wait_ge(s_dve, done.value())

            def group(tile, g):
                return tile[..., bass.ds(g * GC, GC)]

            def put_indices(tile, g, h):
                step(V.tensor_scalar(stage_i[:, h, :], tile[:, bass.ds(g * GC, GC)], 0, None, ALU.add))

            def select(a, wanted, twice):
                def consume(g, h):
                    rec4 = stage[:, h, 0:GC * 3 * QUAD].bitcast(I32).rearrange("p (c k q) -> p c k q", k=3, q=QUAD)
                    m, cnt, sel, prod = (match[:, k] for k in range(4))
                    step(V.tensor_tensor(m, rec4[:, :, a, :], node[:, a, bass.ds(g * GC + LEAD, GC)].unsqueeze(2)
                                         .to_broadcast([P, GC, QUAD]), ALU.is_equal))
                    step(V.tensor_scalar(cnt[:, :, 1:2], m[:, :, 0:1], 1.0, None, ALU.mult))
                    step(V.tensor_tensor(cnt[:, :, 2:3], cnt[:, :, 1:2], m[:, :, 1:2], ALU.add))
                    step(V.tensor_tensor(cnt[:, :, 3:4], cnt[:, :, 2:3], m[:, :, 2:3], ALU.add))
                    step(V.tensor_tensor(sel, cnt, twin[:, a, bass.ds(g * GC, GC)].unsqueeze(2)
                                         .to_broadcast([P, GC, QUAD]), ALU.is_equal))
                    step(V.tensor_tensor(sel, sel, m, ALU.mult))
                    for values, target in wanted(rec4, g):
                        step(V.tensor_tensor(prod, sel, values, ALU.mult))
                        step(V.tensor_tensor(prod[:, :, 0:2], prod[:, :, 0:2], prod[:, :, 2:4], ALU.add))
                        step(V.tensor_tensor(target, prod[:, :, 0:1], prod[:, :, 1:2], ALU.add))
                return consume

            def of_a(rec4, g):
                return ((rec4[:, :, 1, :], other[:, 0, bass.ds(g * GC, GC)].unsqueeze(2)),
                        (rec4[:, :, 2, :].bitcast(F32), wgt[:, bass.ds(g * GC, GC)].unsqueeze(2)))

            def of_b(rec4, g):
                return ((rec4[:, :, 0, :], other[:, 1, bass.ds(g * GC, GC)].unsqueeze(2)),
                        (four[:].unsqueeze(1).to_broadcast([P, GC, QUAD]),
                         edge_b[:, bass.ds(g * GC, GC)].unsqueeze(2)))

            one_pass(FIRST["rec_a"], lambda g, h, i: put_indices(quad[:, 0], g, h), select(0, of_a, 2), 12, 1)
            v.sem_inc(s_wsel, 1)
            def find_b():
                one_pass(FIRST["rec_b"], lambda g, h, i: put_indices(quad[:, 1], g, h), select(1, of_b, 2), 12, 1)
                step(V.scalar_tensor_tensor(edge_b[:], quad[:, 1], float(QUAD), edge_b[:], ALU.mult, ALU.add))

            def wait_b():
                v.sem_inc(s_idx, NG)
                for h in range(2):
                    v.wait_ge(s_land[h], (FIRST["rec_b"] // 2 + PAIRS) * LANDED)
                settle()

            otherwise(in_order == 0, find_b, wait_b, 13 * NG + 1)

            def fill_map(g, h, i):
                step(V.tensor_scalar(stage[:, h, 0:GC].bitcast(I32), slot_i[:, bass.ds(g * GC, GC)], N, None, ALU.add))
                put_indices(last_i[:, 0], g, h)

            one_pass(FIRST["map_put"], fill_map, lambda g, h: None, 0, 2)

            def take_map(g, h):
                step(V.tensor_scalar(gidx[:, bass.ds(g * GC, GC)], stage[:, h, 0:GC].bitcast(I32), 0, None, ALU.add))

            def norm_steps(u, np_, target, k, n):
                def bc(a):
                    return a[0:np_].unsqueeze(2).to_broadcast([np_, ROWS, C])
                def centre():
                    step(V.tensor_reduce(u["sum"][0:np_], u["y"][0:np_], AX.X, ALU.add))
                    step(V.tensor_scalar(u["mean"][0:np_], u["sum"][0:np_], 1.0 / C, None, ALU.mult))
                    step(V.tensor_tensor(u["y"][0:np_], u["y"][0:np_], bc(u["mean"]), ALU.subtract))
                    step(V.tensor_tensor(u["sq"][0:np_], u["y"][0:np_], u["y"][0:np_], ALU.mult))
                    step(V.tensor_reduce(u["var"][0:np_], u["sq"][0:np_], AX.X, ALU.add))
                    v.sem_inc(s_var[k], 1)
                def norm():
                    v.wait_ge(s_std[k], n)
                    step(V.reciprocal(u["rstd"][0:np_], u["std"][0:np_]))
                    step(V.tensor_tensor(target, u["y"][0:np_], bc(u["rstd"]), ALU.mult))
                    v.sem_inc(s_res[k], 1)
                return centre, norm

            for h in range(2):
                step(V.memset(d1[h]["o"][:, :, C:AW], 1.0))
            v.sem_inc(s_go1, 1)

            def x_blocks(n, np_, hs):
                parts = []
                for h in hs:
                    u = d1[h]
                    v.wait_ge(s_in[0][h], n * 16 + 16)
                    step(V.tensor_scalar(u["y"][0:np_], u["y"][0:np_], 2.0, None, ALU.mult))
                    parts.append(norm_steps(u, np_, u["o"][0:np_, :, 0:C], 0, n * 2 + (h + 1)))
                    parts[-1][0]()
                for _, norm in parts:
                    norm()

            def x_beside(base):
                def beside(i):
                    for j in range(NB // 2 // (2 * (PAIRS - 1))):
                        x_blocks(i * (NB // 2 // (2 * (PAIRS - 1))) + (base + j), P, (0, 1))
                return beside

            PER_PASS = NB // 4
            BESIDE = 2 * 8 * (NB // 2 // (2 * (PAIRS - 1)))
            assert NB // 2 == 2 * (PAIRS - 1) * (NB // 2 // (2 * (PAIRS - 1)))
            one_pass(FIRST["map_get"], lambda g, h, i: put_indices(other[:, 0], g, h), take_map, 1, 1,
                     x_beside(0), BESIDE)
            for h in range(2):
                step(V.tensor_copy(gidx[:, COLS + h * GC:COLS + (h + 1) * GC], gidx[:, h * GC:(h + 1) * GC]))

            def stage_rows(h):
                return stage[:, h, 0:GC * C].rearrange("p (c f) -> p c f", f=C)

            def rows_of(g):
                return rows[:, bass.ds(g, 1)].rearrange("p o c f -> p (o c) f")

            def take_rows(g, h):
                step(V.tensor_scalar(rows_of(g), stage_rows(h), 1.0, None, ALU.mult))
                v.sem_inc(s_rows, 1)

            v.wait_ge(s_mapd, 16)
            v.wait_ge(s_aggd, 16)
            def put_sources(g, h, i):
                step(V.tensor_scalar(stage_i[:, h, :], node[:, 0, bass.ds(g * GC + LEAD, GC)], float(N - 1), None, ALU.min))

            one_pass(FIRST["first"], put_sources, take_rows, 1, 1, x_beside(PER_PASS), BESIDE)
            x_blocks(NB // 2, TAILP, (0,))

            win = window[:].rearrange("p (f w) -> p f w", w=WIN)

            def carry_in(g):
                step(V.tensor_scalar(win[:, :, 0:1],
                                     runs[:, bass.ds(g * FLAT, FLAT)].rearrange("p (f w) -> p f w", w=WIN)[:, :, GC:WIN],
                                     1.0, None, ALU.mult))

            def scan_forward(g, op0, op1):
                step(v.tensor_tensor_scan(runs[:, bass.ds(g * FLAT + FLAT, FLAT)], joined[:, bass.ds(g * FLAT, FLAT)],
                                          window[:], 0.0, op0, op1))

            def rises(g, h):
                step(V.tensor_tensor(diff[:], stage_rows(h), rows_of(g), ALU.subtract))
                carry_in(g)
                step(V.scalar_tensor_tensor(win[:, :, 1:].rearrange("p f c -> p c f"), diff[:], 0.0,
                                            wgt[:, bass.ds(g * GC, GC)].unsqueeze(2).to_broadcast([P, GC, C]),
                                            ALU.max, ALU.mult))
                scan_forward(g, ALU.min, ALU.max)

            def run_win(g):
                return runs[:, bass.ds(g * FLAT + FLAT, FLAT)].rearrange("p (f w) -> p f w", w=WIN)

            def apply(g, m, w0, w1, op0, op1):
                n = w1 - w0
                step(V.tensor_tensor(fix[:, :, 0:n],
                                     cross[:, m, bass.ds(g * GC + w0, n)].unsqueeze(1).to_broadcast([P, C, n]),
                                     ps_small[:, 2 * P:2 * P + C].unsqueeze(2).to_broadcast([P, C, n]), op0))
                step(V.tensor_tensor(run_win(g)[:, :, w0:w1], run_win(g)[:, :, w0:w1], fix[:, :, 0:n], op1))

            def over_partitions(m, backward, op0, op1):
                ask()
                if backward:
                    step(v.tensor_tensor_scan(ends_t[:, 1, 0:P][:, ::-1],
                                              whole[:, m, ::-1], ps_small[0:C, 0:P][:, ::-1], 0.0, op0, op1))
                else:
                    step(v.tensor_tensor_scan(ends_t[:, 0, 1:P + 1], whole[:, m, :], ps_small[0:C, 0:P], 0.0, op0, op1))
                ask()
                if backward:
                    near, far = (NG - 1, WIN - NEAR, WIN), (NG - 1, 1, WIN - NEAR)
                    rest, w0 = (0, NG - 1), 1
                else:
                    near, far = (0, 1, 1 + NEAR), (0, 1 + NEAR, WIN)
                    rest, w0 = (1, NG), 0
                apply(near[0], m, near[1], near[2], op0, op1)
                before_if = done.n
                far_steps = 2 + 2 * (rest[1] - rest[0])
                settle()
                with v.If(long_runs):
                    apply(far[0], m, far[1], far[2], op0, op1)
                    settle()
                    with v.Fori(0, rest[1] - rest[0]) as g:
                        start = done.enter(g, 2)
                        apply(g + rest[0], m, w0, WIN, op0, op1)
                        settle()
                        done.leave(start, rest[1] - rest[0])
                with v.Else():
                    v.sem_inc(s_dve, far_steps)
                assert done.n - before_if == far_steps
                v.wait_ge(s_dve, done.value())

            def scan_backward(g):
                at = (g + 1) * FLAT
                step(v.tensor_tensor_scan(runs[:, at:at + FLAT][:, ::-1], joined[:, g * FLAT + 1:(g + 1) * FLAT + 1][:, ::-1],
                                          runs[:, at:at + FLAT][:, ::-1], 0.0, ALU.min, ALU.max))

            def new_rows(target, g, cols=GC):
                step(V.tensor_tensor(target, rows_of(g)[:, 0:cols], run_win(g)[:, :, 1:1 + cols]
                                     .rearrange("p f c -> p c f"), ALU.add))

            v.wait_ge(s_sqrt, 1)
            for h in range(2):
                v.wait_ge(s_resd[0][h], 16 * (NB // 2 + (1 if h == 0 else 0)))
            v.wait_ge(s_firstd, 16 * NG)
            v.wait_ge(s_neard, 16)
            step(V.memset(runs[:, 0:FLAT], 0.0))
            for h in range(2):
                put_indices(gidx, h, h)
                v.sem_inc(s_idx, 1)
            settle()
            with v.Fori(0, ITERATIONS // 2) as it:
                per = 2 * (NG * 6 + (3 + 2 * NG) + NG + 1 + (1 + 2 * (NG - 1)) + (3 + 2 * NG) + NG)
                start = done.enter(it, per)
                astart, bstart = asks.enter(it, 8), answers.enter(it, 8)
                for half in range(2):
                    settle()
                    with v.Fori(0, PAIRS) as i:
                        inner = done.enter(i, 2 * 6)
                        for h in range(2):
                            g = i * 2 + h
                            v.wait_ge(s_land[h], it * (NG * LANDED) + i * LANDED
                                      + ((FIRST["round"] + half * NG) // 2 + 1) * LANDED)
                            rises(g, h)
                            put_indices(gidx, g + 2, h)
                            v.sem_inc(s_idx, 1)
                            v.wait_ge(s_tabled[h], it * (2 * PAIRS * 16) + i * 16 + 16 * PAIRS * (half + 1))
                            new_rows(tbuf[:, h], g)
                            v.sem_inc(s_table, 1)
                        settle()
                        done.leave(inner, PAIRS)
                    over_partitions(0, False, ALU.min, ALU.max)

                    def store_again():
                        for h in range(2):
                            v.wait_ge(s_tabled[h], it * (2 * PAIRS * 16) + 16 * PAIRS * (half + 2))
                        settle()
                        with v.Fori(0, NG) as g:
                            inner = done.enter(g, 1)
                            new_rows(tbuf[:, 0], g)
                            v.sem_inc(s_again, 1)
                            v.wait_ge(s_againd, it * (2 * NG * 16) + g * 16 + 16 * (half * NG + 1))
                            settle()
                            done.leave(inner, NG)

                    otherwise(long_runs, store_again, lambda: None, NG)
                    v.wait_ge(s_tabled[0], it * (2 * PAIRS * 16) + 16 * PAIRS * (half + 2))
                    v.wait_ge(s_neard, it * 32 + 16 * (half + 1))
                    new_rows(near_rows[:], 0, NEAR)
                    v.sem_inc(s_near, 1)
                    scan_backward(NG - 1)
                    for g in reversed(range(NG - 1)):
                        step(V.tensor_scalar(run_win(g)[:, :, GC:WIN], run_win(g + 1)[:, :, 0:1], 1.0, None, ALU.mult))
                        scan_backward(g)
                    over_partitions(1, True, ALU.min, ALU.max)
                    settle()
                    with v.Fori(0, NG) as g:
                        inner = done.enter(g, 1)
                        new_rows(rows_of(g), g)
                        settle()
                        done.leave(inner, NG)
                settle()
                done.leave(start, ITERATIONS // 2)
                asks.leave(astart, ITERATIONS // 2)
                answers.leave(bstart, ITERATIONS // 2)

            for h in range(2):
                v.wait_ge(s_tabled[h], 16 * PAIRS * (ITERATIONS + 1))
            v.sem_inc(s_xfree, 2)
            square = window[:, 0:GC * C].rearrange("p (c f) -> p c f", f=C)

            def bcg(k):
                return stats[:, k].unsqueeze(2).to_broadcast([P, GC, C])

            def stage_wide(h):
                return stage[:, h, :].rearrange("p (c f) -> p c f", f=AW)

            def fill_norm(g, h, i):
                v.wait_ge(s_xin[h], i * 16 + 16)
                step(V.tensor_tensor(diff[:], tbuf[:, h], rows_of(g), ALU.add))
                v.sem_inc(s_xfree, 1)
                step(V.tensor_reduce(stats[:, 0], diff[:], AX.X, ALU.add))
                step(V.tensor_scalar(stats[:, 1], stats[:, 0], 1.0 / C, None, ALU.mult))
                step(V.tensor_tensor(diff[:], diff[:], bcg(1), ALU.subtract))
                step(V.tensor_tensor(square, diff[:], diff[:], ALU.mult))
                step(V.tensor_reduce(stats[:, 2], square, AX.X, ALU.add))
                v.sem_inc(s_nvar, 1)
                v.wait_ge(s_nstd, g + 1)
                step(V.reciprocal(stats[:, 4], stats[:, 3]))
                step(V.tensor_tensor(stage_wide(h)[:, :, 0:C], diff[:], bcg(4), ALU.mult))
                step(V.tensor_scalar(stage_wide(h)[:, :, C:AW], degree_root[:, bass.ds(g * GC, GC)].unsqueeze(2),
                                     1.0, None, ALU.mult))
                put_indices(last_i[:, 0], g, h)

            one_pass(FIRST["final_put"], fill_norm, lambda g, h: None, 0, 10)
            def take_attr(g, h):
                step(V.tensor_scalar(rows_of(g), stage_rows(h), 1.0, None, ALU.mult))

            def gather_attr():
                one_pass(FIRST["attr"], lambda g, h, i: put_indices(edge_b, g, h), take_attr, 1, 1)

            def wait_attr():
                v.sem_inc(s_idx, NG)
                settle()

            otherwise(in_order == 0, gather_attr, wait_attr, 2 * NG)
            step(V.memset(joined[:], 0.0))
            build_masks(1, 1.0)

            def messages(g, h):
                carry_in(g)
                step(V.tensor_tensor(diff[:], stage_wide(h)[:, :, 0:C],
                                     stage_wide(h)[:, :, C:AW].to_broadcast([P, GC, C]), ALU.mult))
                step(V.tensor_tensor(win[:, :, 1:].rearrange("p f c -> p c f"), diff[:], rows_of(g), ALU.add))
                scan_forward(g, ALU.mult, ALU.add)

            one_pass(FIRST["x1_get"], lambda g, h, i: put_indices(other[:, 1], g, h), messages, 4, 1)
            over_partitions(2, False, ALU.mult, ALU.add)

            def fill_sums(g, h, i):
                step(V.tensor_scalar(stage_wide(h)[:, :, 0:C], run_win(g)[:, :, 1:].rearrange("p f c -> p c f"), 1.0, None, ALU.mult))
                step(V.tensor_scalar(stage_wide(h)[:, :, C:AW], length[:, 1, bass.ds(g * GC, GC)].unsqueeze(2), 1.0, None, ALU.mult))
                put_indices(last_i[:, 1], g, h)

            one_pass(FIRST["agg_put"], fill_sums, lambda g, h: None, 0, 3)
            v.sem_inc(s_go2, 1)

            def blocks(i, np_, hs):
                first = i * 2
                norms = {}
                for h in hs:
                    u = d2[h]
                    v.wait_ge(s_in[1][h], i * 32 + 32)
                    step(V.tensor_copy(u["deg"][0:np_], u["agg"][0:np_, :, C]))
                    v.sem_inc(s_var[1], 1)
                for h in hs:
                    u = d2[h]
                    v.wait_ge(s_std[1], i * 4 + (h + 1))
                    step(V.reciprocal(u["mean"][0:np_], u["deg"][0:np_]))
                    step(V.tensor_tensor(u["f"][0:np_], u["agg"][0:np_, :, 0:C],
                                         u["mean"][0:np_].unsqueeze(2).to_broadcast([np_, ROWS, C]), ALU.mult))
                    v.sem_inc(s_scaled, 1)
                    step(V.tensor_tensor(u["sq"][0:np_], u["x"][0:np_, :, 0:C],
                                         bias_b[0:np_].unsqueeze(1).to_broadcast([np_, ROWS, C]), ALU.add))
                for h in hs:
                    u = d2[h]
                    v.wait_ge(s_mm, first + (h + 1))
                    step(V.tensor_tensor(u["y"][0:np_], ps_y[h][0:np_].rearrange("p (r f) -> p r f", f=C),
                                         u["sq"][0:np_], ALU.add))
                    v.sem_inc(s_mmfree, 1)
                    norms[h] = norm_steps(u, np_, u["f"][0:np_], 1, i * 4 + (len(hs) + h + 1))
                    norms[h][0]()
                for h in hs:
                    norms[h][1]()

            settle()
            with v.Fori(0, NB // 2) as i:
                start = done.enter(i, 2 * 12)
                blocks(i, P, (0, 1))
                settle()
                done.leave(start, NB // 2)
            blocks(NB // 2, TAILP, (0,))


_INS = ["x", "src", "dst", "edge_attr_32", "edge_weight", "L1_gnn_weight", "L1_gnn_bias"]


def kernel(**inputs):
    import numpy as _np
    import concourse.bacc as _bacc
    from concourse import mybir as _mybir
    from concourse.bass_utils import run_bass_kernel_spmd as _run

    nc = _bacc.Bacc("TRN2", target_bir_lowering=False, num_devices=1)
    arrays, args = {}, []
    for name in _INS:
        a = _np.ascontiguousarray(inputs[name])
        arrays[f"in_{name}_dram"] = a
        args.append(nc.dram_tensor(f"in_{name}_dram", a.shape, _mybir.dt.from_np(a.dtype), kind="ExternalInput").ap())
    shape = arrays["in_x_dram"].shape
    args.append(nc.dram_tensor("out_0_dram", shape, _mybir.dt.float32, kind="ExternalOutput").ap())
    resnorm_gnn(nc, *args)
    r = _run(nc, [arrays], core_ids=[0])
    return r.results[0]["out_0_dram"]
```

```python
from contextlib import ExitStack

import concourse.bass as bass
from concourse import mybir

ALU = mybir.AluOpType
ACT = mybir.ActivationFunctionType
AX = mybir.AxisListType
F32 = mybir.dt.float32
I32 = mybir.dt.int32

P = 128
GC = 28
QUAD = 4
BIG = 3.0e38
KEY_SHIFT = 14
KEY_OFFSET = 512
ITERATIONS = 10
EPS = 1e-5
NEAR = 8
ROWS = 16


class Count:

    def __init__(self, sem, step=1):
        self.sem, self.step, self.n, self.loops = sem, step, 0, []

    def inc(self, instruction):
        self.n += 1
        return instruction.then_inc(self.sem, self.step)

    def value(self):
        v = self.n * self.step
        for i, per in self.loops:
            v = i * (per * self.step) + v
        return v

    def enter(self, i, per):
        self.loops.append((i, per))
        return self.n

    def leave(self, start, trips):
        _, per = self.loops.pop()
        assert self.n - start == per, (self.n - start, per)
        self.n = start + per * trips


def resnorm_gnn(nc, x, src, dst, edge_attr, edge_weight, weight, bias, out, debug=None):
    N, C = x.shape
    E = src.shape[0]
    SIDE = 512
    COLS = -(-E // (P * 2 * GC)) * 2 * GC
    NG = COLS // GC
    SLOTS = P * COLS
    SORTED = P * SIDE
    ER = 100
    EC = E // ER
    LEAD = 16
    KW = LEAD + COLS + LEAD
    WIN = GC + 1
    FLAT = C * WIN
    assert E == ER * EC and EC % QUAD == 0 and EC <= SIDE and NG % 2 == 0 and SLOTS <= SORTED
    assert N + KEY_OFFSET + (SORTED - E) < 1 << 17 and E // QUAD < 1 << KEY_SHIFT
    BUFS = 4
    BLOCK = P * ROWS
    NB = N // BLOCK
    TAILP = (N - NB * BLOCK) // ROWS
    assert NB % BUFS == 0 and NB * BLOCK + TAILP * ROWS == N
    AW = C + 1

    def scratch(name, shape, dt):
        kind = "ExternalOutput" if debug and name in debug else "Internal"
        return nc.dram_tensor(name, shape, dt, kind=kind).ap()

    keys_d = scratch("keys_d", [2, LEAD + SORTED], I32)
    rec_d = scratch("rec_d", [E // QUAD, 3 * QUAD], I32)
    XREC = QUAD * (C + 3)
    xrec_d = scratch("xrec_d", [SLOTS // QUAD, XREC], F32)
    xmap_d = scratch("xmap_d", [N, AW], F32)
    table_d = [scratch("table0_d", [N + SLOTS, C], F32), scratch("table1_d", [N + SLOTS, C], F32)]
    first_d = scratch("first_d", [SLOTS, C], F32)
    x1_d = scratch("x1_d", [N, AW], F32)
    dst_d = scratch("dst_d", [SLOTS], I32)
    src_d = scratch("src_d", [SLOTS], I32)
    attr_d = scratch("attr_d", [SLOTS, C], F32)
    agg_d = scratch("agg_d", [N, C], F32)

    with ExitStack() as ctx:
        def sb(name, shape, dt):
            return ctx.enter_context(nc.sbuf_tensor(name, shape, dt))

        def psum(name, shape, dt):
            return ctx.enter_context(nc.psum_tensor(name, shape, dt))

        def sem(name):
            return ctx.enter_context(nc.semaphore(name))

        runs = sb("runs", [P, (NG + 1) * FLAT], F32)
        joined = sb("joined", [P, NG * FLAT + 1], F32)
        rows = sb("rows", [P, NG, GC, C], F32)
        stage = sb("stage", [P, 2, GC * AW], F32)
        stage_i = sb("stage_i", [P, 2, GC], I32)
        window = sb("window", [P, FLAT], F32)
        diff = sb("diff", [P, GC, C], F32)
        node = sb("node", [P, 2, KW], F32)
        other = sb("other", [P, 2, COLS], I32)
        edge_b = sb("edge_b", [P, COLS], I32)
        wgt = sb("wgt", [P, COLS], F32)
        gidx = sb("gidx", [P, COLS + 2 * GC], I32)
        tbuf = sb("tbuf", [P, 2, GC, C], F32)
        near_rows = sb("near_rows", [P, NEAR, C], F32)
        stats = sb("stats", [P, 5, GC], F32)
        last_i = sb("last_i", [P, 2, COLS], I32)
        length = sb("length", [P, 2, COLS], F32)
        slot_i = sb("slot_i", [P, COLS], I32)
        ident = sb("ident", [P, P], F32)
        small = sb("small", [P, 64], F32)
        small_i = sb("small_i", [P, 8], I32)
        four = sb("four", [P, QUAD], F32)
        cross = sb("cross", [P, 3, 1 + COLS], F32)
        cross_col = sb("cross_col", [P, 3, C], F32)
        whole = sb("whole", [C, 3, P], F32)
        ends_t = sb("ends_t", [C, 2, P + 1], F32)
        flags = sb("flags", [1, 2], I32)
        pads = sb("pads", [2, SLOTS - E], I32)
        zero_i = sb("zero_i", [2, LEAD], I32)
        wblk = sb("wblk", [P, P], F32)
        bias_b = sb("bias_b", [P, C], F32)

        AP0Z = 88
        assert (SLOTS - E) * C % AP0Z == 0
        def part(tile, start, shape, dt=F32):
            size = 1
            for n in shape:
                size *= n
            v = tile[:, start:start + size]
            if dt is not F32:
                v = v.bitcast(dt)
            if len(shape) == 2:
                v = v.rearrange("p (a b) -> p a b", a=shape[0])
            if len(shape) == 3:
                v = v.rearrange("p (a b c) -> p a b c", a=shape[0], b=shape[1])
            return v

        W2 = 2 * SIDE
        sort_buf = [runs[:, 0:W2], runs[:, W2:2 * W2]]
        turn_buf = [runs[:, 2 * W2:3 * W2], runs[:, 3 * W2:4 * W2]]
        raw_edges = part(runs, 4 * W2, [2, EC], I32)
        raw_w = part(runs, 4 * W2 + 2 * EC, [EC])
        quarter = part(runs, 4 * W2 + 3 * EC, [EC], I32)
        rec = part(runs, 4 * W2 + 4 * EC, [EC // QUAD, 3, QUAD], I32)
        TEMP = 4 * W2 + 7 * EC
        same = part(runs, TEMP, [2, COLS])
        match = part(runs, TEMP + 2 * COLS, [4 * GC * QUAD]).rearrange("p (k c q) -> p k c q", k=4, q=QUAD)
        dst_slots = part(runs, TEMP + 2 * COLS + 4 * GC * QUAD, [COLS], I32)
        line = part(runs, TEMP + 3 * COLS + 4 * GC * QUAD, [4, P + 1])[0:1]
        assert TEMP + 3 * COLS + 4 * GC * QUAD + 4 * (P + 1) <= NG * FLAT
        zeros = part(joined, 0, [(SLOTS - E) * C // AP0Z])
        rows_flat = rows[:].rearrange("p g c f -> p (g c f)")
        XP, XR = 125, 40
        CHUNKS = N // (XP * XR)
        numbers_i = part(rows_flat, 0, [CHUNKS, XR], I32)
        numbers = part(rows_flat, CHUNKS * XR, [CHUNKS, XR])
        AP0, AR = 80, 25
        agg_rows = part(rows_flat, 2 * CHUNKS * XR, [AR, C])
        KA = 2 * CHUNKS * XR + AR * C
        keys = part(rows_flat, KA, [2, KW], I32)
        quad = part(rows_flat, KA + 2 * KW, [2, COLS], I32)
        twin = part(rows_flat, KA + 2 * KW + 2 * COLS, [2, COLS])
        XAT = KA + 2 * KW + 4 * COLS
        x_in = [part(rows_flat, XAT + k * XR * C, [XR, C]) for k in range(2)]
        x_wide = [part(rows_flat, XAT + 2 * XR * C + k * XR * AW, [XR, AW]) for k in range(2)]
        assert CHUNKS % 2 == 0 and CHUNKS * XP * XR == N and XAT + 2 * XR * (C + AW) <= NG * GC * C
        stage_x = [joined[:, k * GC * XREC:(k + 1) * GC * XREC] for k in range(2)]
        index_x = [edge_b[:, k * GC:(k + 1) * GC] for k in range(2)]
        assert 2 * GC * XREC <= NG * FLAT and N % (AP0 * AR) == 0

        fix = window[:].rearrange("p (f w) -> p f w", w=WIN)

        DW = ROWS * C

        def dense_tiles(tile, h, shapes):
            size = sum(s[0] * (s[1] if len(s) > 1 else 1) for s in shapes.values())
            at, t = h * size, {}
            for name, shape in shapes.items():
                t[name] = part(tile, at, shape)
                at += shape[0] * (shape[1] if len(shape) > 1 else 1)
            return t, at
        norm_shapes = {"y": [ROWS, C], "sq": [ROWS, C], "sum": [ROWS], "mean": [ROWS], "var": [ROWS], "std": [ROWS],
                       "rstd": [ROWS]}
        d1, d2 = [], []
        for h in range(2):
            t, end1 = dense_tiles(runs, h, {**norm_shapes, "o": [ROWS, AW]})
            d1.append(t)
        for h in range(BUFS):
            t, end2 = dense_tiles(rows_flat, h, {**norm_shapes, "x": [ROWS, AW], "agg": [ROWS, C], "f": [ROWS, C]})
            d2.append(t)
        assert end1 <= NG * FLAT and end2 <= NG * GC * C and DW == 512
        turned_sum = [part(joined, h * DW, [DW]) for h in range(BUFS)]

        turned_a = psum("turned_a", [P, W2], F32)
        turned_b = psum("turned_b", [P, W2], F32)
        ps_small = psum("ps_small", [P, 512], F32)
        ps_more = psum("ps_more", [P, W2], F32)
        ps_t = [turned_a[:, 0:512], turned_a[:, 512:1024]]
        ps_y = [t[:, k:k + 512] for t in (turned_b, ps_more) for k in (0, 512)]

        s_edges = sem("edges_loaded")
        s_iota = sem("iotas_written")
        s_pooled = sem("pool_steps")
        s_dve = sem("dve_step_done")
        s_quads = sem("quad_records_built")
        s_recd = sem("quad_records_stored")
        s_tabini = sem("first_table_rows_written")
        s_srcd = sem("sources_padded")
        s_xidx = sem("source_indices_copied")
        s_xland = [sem("even_source_rows_landed"), sem("odd_source_rows_landed")]
        s_xrecd = [sem("even_source_rows_stored"), sem("odd_source_rows_stored")]
        s_rowsfree = sem("quads_no_longer_read")
        s_rowsin = sem("source_rows_loaded")
        s_xload = [sem(f"x_chunk_{k}_loaded") for k in range(2)]
        s_numbers = sem("row_numbers_written")
        s_xmade = sem("x_chunk_widened")
        s_xmapd = [sem(f"wide_x_chunk_{k}_stored") for k in range(2)]
        s_aggd = sem("sums_initialised")
        s_xcopy = sem("x_copied_to_tables")
        s_padded = sem("inputs_padded")
        s_padt = sem("pad_tiles_written")
        s_dsts = sem("dst_slots_loaded")
        s_flags = sem("flags_written")
        s_toturn = sem("sort_tiles_to_turn")
        s_turned = sem("sort_tiles_turned")
        s_sorted = sem("keys_sorted")
        s_keysd = sem("keys_stored")
        s_keys = sem("keys_loaded")
        s_wsel = sem("weights_selected")
        s_sqrt = sem("weights_rooted")
        s_ask = sem("small_turn_wanted")
        s_ans = sem("small_turn_done")
        s_idx = sem("indices_ready")
        s_land = [sem("even_stage_landed"), sem("odd_stage_landed")]
        s_idxb = [sem("order_b_record_indices_ready"), sem("feature_indices_ready")]
        s_landb = [[sem(f"{what}_{h}_landed") for h in range(2)] for what in ("order_b_records", "features")]
        s_free = sem("rows_free_for_features")
        s_srcin = sem("sources_loaded")
        s_attrin = sem("features_loaded")
        s_rows = sem("source_rows_selected")
        s_table = sem("table_rows_ready")
        s_tabled = [sem("even_table_rows_stored"), sem("odd_table_rows_stored")]
        s_near = sem("near_rows_ready")
        s_neard = sem("near_rows_stored")
        s_again = sem("long_run_rows_ready")
        s_againd = sem("long_run_rows_stored")
        s_xfree = sem("norm_buffer_free")
        s_xin = [sem("even_norm_rows_loaded"), sem("odd_norm_rows_loaded")]
        s_nvar = sem("norm_variance_ready")
        s_nstd = sem("norm_deviation_ready")
        s_deg = sem("out_degrees_ready")
        s_degroot = sem("out_degrees_rooted")
        s_gate = sem("pool_gate_passed")
        s_go1 = sem("block_buffers_usable")
        s_go2 = sem("layer1_sums_all_landed")
        s_weights = sem("weights_loaded")
        s_in = [sem(f"x_block_{h}_loaded") for h in range(2)]
        s_res = sem("x_block_result_ready")
        s_resd = [sem(f"x_block_{h}_stored") for h in range(2)]
        s_var = sem("x_block_variance_ready")
        s_std = sem("x_block_deviation_ready")
        s_sumin = [sem(f"sums_{h}_loaded") for h in range(BUFS)]
        s_x1in = [sem(f"layer0_rows_{h}_loaded") for h in range(BUFS)]
        s_biased = sem("bias_added")
        s_centred = sem("last_block_centred")
        s_squared = sem("last_block_squared")
        s_lvar = sem("last_block_variance_ready")
        s_lstd = sem("last_block_deviation_ready")
        s_lres = sem("last_block_result_ready")
        s_lresd = [sem(f"last_block_{h}_stored") for h in range(BUFS)]
        s_pegate = sem("pe_gate_passed")
        s_spgate = sem("sp_gate_passed")
        s_settled = sem("dve_wait_ended")
        s_sumt = sem("sums_turned")
        s_sumc = sem("turned_sums_copied")
        s_mm = sem("products_ready")
        s_mmfree = sem("products_read")

        block = ctx.enter_context(nc.Block())

        PASSES = ["rec_a", "map_put"] + ["round"] * ITERATIONS + ["final_put", "x1_get", "agg_put"]
        FIRST = {}
        for k, name in enumerate(PASSES):
            FIRST.setdefault(name, k * NG)
        LANDED = 16 * GC
        PAIRS = NG // 2

        LOOPED = (ITERATIONS - 2) // 2
        assert ITERATIONS == 2 * LOOPED + 2
        PIECES, PR = 10, 125
        assert N % (PIECES * PR) == 0
        table_slots = [t[N:N + SLOTS, :].rearrange("(p c) f -> p c f", p=P) for t in table_d]

        def run_column(g, w):
            return runs[:, (g + 1) * FLAT:(g + 2) * FLAT].rearrange("p (f w) -> p f w", w=WIN)[:, :, w]

        @block.sync
        def _(sp):
            sp.dma_start(raw_edges[0:ER, 0, :], src.rearrange("(p c) -> p c", p=ER)).then_inc(s_edges, 16)
            sp.dma_start(raw_edges[0:ER, 1, :], dst.rearrange("(p c) -> p c", p=ER)).then_inc(s_edges, 16)
            sp.dma_start(raw_w[0:ER], edge_weight.rearrange("(p c) -> p c", p=ER)).then_inc(s_edges, 16)
            sp.wait_ge(s_srcd, 32)
            sp.dma_start(other[:, 1], src_d.rearrange("(p c) -> p c", p=P)).then_inc(s_srcin, 16)
            sp.wait_ge(s_tabini, 1)
            pieces = N // (AP0 * AR)
            sp.dma_start(agg_d.rearrange("(p k r) f -> p k (r f)", p=AP0, k=pieces),
                         agg_rows[0:AP0].rearrange("p a b -> p (a b)").unsqueeze(1)
                         .to_broadcast([AP0, pieces, AR * C])).then_inc(s_aggd, 16)
            sp.wait_ge(s_quads, 1)
            sp.dma_start(rec_d.rearrange("(p c) f -> p (c f)", p=ER),
                         rec[0:ER].rearrange("p a b c -> p (a b c)")).then_inc(s_recd, 16)
            sp.dma_start(xrec_d[0:E // QUAD, QUAD * C:XREC].rearrange("(p c) f -> p c f", p=ER),
                         rec[0:ER].rearrange("p a b c -> p a (b c)").bitcast(F32)).then_inc(s_recd, 16)
            sp.wait_ge(s_sorted, 1)
            sp.dma_start(keys_d[:, 0:LEAD], zero_i[:]).then_inc(s_keysd, 16)
            for a in range(2):
                sp.dma_start(keys_d[a, LEAD:LEAD + SORTED].rearrange("(p c) -> p c", p=P),
                             sort_buf[0][:, a * SIDE:(a + 1) * SIDE].bitcast(I32)).then_inc(s_keysd, 16)
            sp.wait_ge(s_keysd, 48)
            for a in range(2):
                around = bass.AP(keys_d.tensor, a * (LEAD + SORTED), [[COLS, P], [1, KW]])
                sp.dma_start(keys[:, a, :], around).then_inc(s_keys, 16)
            sp.wait_ge(s_padded, 64)
            sp.dma_start(dst_slots, dst_d.rearrange("(p c) -> p c", p=P)).then_inc(s_dsts, 16)
            sp.wait_ge(s_flags, 1)
            sp.sem_inc(s_spgate, 1)
            long_runs = sp.value_load(flags[0:1, 0:1], min_val=0, max_val=SLOTS) > NEAR
            in_order = sp.value_load(flags[0:1, 1:2], min_val=0, max_val=1)

            kept = first_d.rearrange("(p c) f -> p c f", p=P)
            with sp.Fori(0, PAIRS) as i:
                for h in range(2):
                    g = i * 2 + h
                    sp.wait_ge(s_rows, g + 1)
                    sp.dma_start(kept[:, bass.ds(g * GC, GC), :], tbuf[:, h]).then_inc(s_tabled[h], 16)
            for h in range(2):
                sp.wait_ge(s_tabled[h], PAIRS * 16)
                sp.wait_ge(s_xmapd[h], CHUNKS // 2 * 16)
            sp.wait_ge(s_aggd, 16)
            sp.wait_ge(s_rowsfree, 1)
            sp.dma_start(rows_flat, first_d.rearrange("(p c) f -> p (c f)", p=P)).then_inc(s_rowsin, 16)
            def store_rows(k, table):
                with sp.Fori(0, PAIRS) as i:
                    for h in range(2):
                        sp.wait_ge(s_table, k * NG + i * 2 + (h + 1))
                        sp.dma_start(table[:, bass.ds((i * 2 + h) * GC, GC), :], tbuf[:, h]).then_inc(s_tabled[h], 16)
                with sp.If(long_runs):
                    with sp.Fori(0, NG) as g:
                        sp.wait_ge(s_again, k * NG + g + 1)
                        sp.dma_start(table[:, bass.ds(g * GC, GC), :], tbuf[:, 0]).then_inc(s_againd, 16)
                sp.wait_ge(s_near, k + 1)
                sp.dma_start(table[:, 0:NEAR, :], near_rows[:]).then_inc(s_neard, 16)

            store_rows(0, table_slots[1])
            with sp.Fori(0, LOOPED) as it:
                for half in range(2):
                    store_rows(it * 2 + (half + 1), table_slots[half])

            with sp.Fori(0, PAIRS) as i:
                for h in range(2):
                    sp.wait_ge(s_xfree, i * 2 + h + 1)
                    sp.dma_start(tbuf[:, h], kept[:, bass.ds((i * 2 + h) * GC, GC), :]).then_inc(s_xin[h], 16)

            with sp.If(in_order != 0):
                sp.wait_ge(s_free, 1)
                sp.sem_inc(s_spgate, 1)
                sp.dma_start(rows_flat, attr_d.rearrange("(p c) f -> p (c f)", p=P)).then_inc(s_attrin, 16)

            def load_sums(h, np_, lo):
                sp.dma_start(d2[h]["agg"][0:np_].rearrange("p a b -> p (a b)"),
                             agg_d[bass.ds(lo, np_ * ROWS), :].rearrange("(p r) f -> p (r f)", r=ROWS)
                             ).then_inc(s_sumin[h], 16)

            def load_x1(h, np_, lo):
                sp.dma_start(d2[h]["x"][0:np_].rearrange("p a b -> p (a b)"),
                             x1_d[bass.ds(lo, np_ * ROWS), :].rearrange("(p r) f -> p (r f)", r=ROWS)
                             ).then_inc(s_x1in[h], 16)

            sp.wait_ge(s_go2, 1)
            for h in range(BUFS):
                load_sums(h, P, h * BLOCK)
                load_x1(h, P, h * BLOCK)
            with sp.Fori(1, NB // BUFS) as i:
                for h in range(BUFS):
                    sp.wait_ge(s_sumt, i * BUFS + (h + 1 - BUFS))
                    load_sums(h, P, i * (BUFS * BLOCK) + h * BLOCK)
                    sp.wait_ge(s_mmfree, i * BUFS + (h + 1))
                    load_x1(h, P, i * (BUFS * BLOCK) + h * BLOCK)
            sp.wait_ge(s_sumt, NB + 1 - BUFS)
            load_sums(0, TAILP, NB * BLOCK)
            sp.wait_ge(s_mmfree, NB + 1)
            load_x1(0, TAILP, NB * BLOCK)
            for h in range(BUFS):
                sp.wait_ge(s_lresd[h], (NB // BUFS + (1 if h == 0 else 0)) * 16)

        @block.gpsimd
        def _(pool):
            nc.gpsimd.iota(sort_buf[0].bitcast(I32).rearrange("p (a c) -> p a c", a=2)[:, :, 0:EC],
                           [[0, 2], [1, EC]], base=N + KEY_OFFSET + P * (SIDE - EC) - ER * EC,
                           channel_multiplier=EC).then_inc(s_iota, 1)
            nc.gpsimd.iota(sort_buf[0].bitcast(I32).rearrange("p (a c) -> p a c", a=2)[:, :, EC:SIDE],
                           [[0, 2], [1, SIDE - EC]], base=N + KEY_OFFSET,
                           channel_multiplier=SIDE - EC).then_inc(s_iota, 1)
            nc.gpsimd.iota(quarter, [[1, EC // QUAD], [0, QUAD]], base=0,
                           channel_multiplier=EC // QUAD).then_inc(s_iota, 1)
            nc.gpsimd.iota(slot_i[:], [[1, COLS]], base=0, channel_multiplier=COLS).then_inc(s_iota, 1)
            nc.gpsimd.iota(small_i[:, 0:1], [[0, 1]], base=0, channel_multiplier=1).then_inc(s_iota, 1)
            nc.gpsimd.memset(ident[:], 0.0).then_inc(s_pooled, 1)
            pool.wait_ge(s_pooled, 1)
            nc.gpsimd.affine_select(out=ident[:], in_=ident[:], compare_op=ALU.not_equal, fill=1.0, base=0,
                                    pattern=[[-1, P]], channel_multiplier=1).then_inc(s_iota, 1)
            nc.gpsimd.iota(numbers_i[0:XP], [[XP * XR, CHUNKS], [1, XR]], base=0,
                           channel_multiplier=XR).then_inc(s_pooled, 1)
            pool.wait_ge(s_pooled, 2)
            pool.sem_inc(s_numbers, 1)
            nc.gpsimd.memset(agg_rows[0:AP0], 0.0).then_inc(s_pooled, 1)
            pool.wait_ge(s_pooled, 3)
            pool.sem_inc(s_tabini, 1)

            def rounds(width, table, first, dt=F32, put=None, idx=s_idx, land=s_land, stages=None):
                with pool.Fori(0, PAIRS) as i:
                    for h in range(2):
                        pool.wait_ge(idx, i * 2 + first + h + 1)
                        pool.sem_inc(s_gate, 1)
                        for c in range(GC):
                            piece = (stages[h] if stages else stage[:, h])[:, c * width:(c + 1) * width]
                            if dt is not F32:
                                piece = piece.bitcast(dt)
                            at = bass.IndirectOffsetOnAxis(ap=stage_i[:, h, c:c + 1], axis=0)
                            if put:
                                nc.gpsimd.indirect_dma_start(table, at, piece, None, bounds_check=put - 1,
                                                             oob_is_err=False).then_inc(land[h], 16)
                            else:
                                nc.gpsimd.indirect_dma_start(piece, None, table, at).then_inc(land[h], 16)

            def source_rows(i, h):
                nc.gpsimd.tensor_copy(index_x[h], other[:, 1, bass.ds(i * (2 * GC) + h * GC, GC)]).then_inc(s_xidx, 1)
                pool.wait_ge(s_xidx, i * 2 + (h + 1))
                pool.sem_inc(s_gate, 1)
                for c in range(GC):
                    nc.gpsimd.indirect_dma_start(stage[:, h, c * C:(c + 1) * C], None, x,
                                                 bass.IndirectOffsetOnAxis(ap=index_x[h][:, c:c + 1], axis=0)
                                                 ).then_inc(s_xland[h], 16)

            pool.wait_ge(s_srcin, 16)
            for h in range(2):
                source_rows(0, h)
            with pool.Fori(1, PAIRS) as i:
                for h in range(2):
                    pool.wait_ge(s_xrecd[h], i * 16)
                    source_rows(i, h)
            for h in range(2):
                pool.wait_ge(s_xrecd[h], PAIRS * 16)
            pool.wait_ge(s_recd, 32)
            pool.wait_ge(s_padded, 64)
            rounds(XREC, xrec_d[0:E // QUAD, :], FIRST["rec_a"], stages=stage_x)
            in_order = pool.value_load(flags[0:1, 1:2], min_val=0, max_val=1)
            with pool.If(in_order == 0):
                rounds(3 * QUAD, rec_d, 0, I32, idx=s_idxb[0], land=s_landb[0])
            for k in range(2):
                pool.wait_ge(s_xmapd[k], CHUNKS // 2 * 16)
            rounds(1, xmap_d.rearrange("n (f o) -> (n f) o", o=1), FIRST["map_put"], put=N * AW)
            for h in range(2):
                pool.wait_ge(s_land[h], (FIRST["round"] // 2) * LANDED)
            rounds(AW, xmap_d, FIRST["round"])
            pool.wait_ge(s_xcopy, 32 * PIECES)

            def iteration(k, table):
                for h in range(2):
                    pool.wait_ge(s_tabled[h], k * (PAIRS * 16) + PAIRS * 16)
                pool.wait_ge(s_neard, k * 16)
                pool.sem_inc(s_gate, 1)
                with pool.Fori(0, PAIRS) as i:
                    for h in range(2):
                        pool.wait_ge(s_idx, k * NG + i * 2 + (FIRST["round"] + h + 1))
                        pool.sem_inc(s_gate, 1)
                        for c in range(GC):
                            nc.gpsimd.indirect_dma_start(
                                stage[:, h, c * C:(c + 1) * C], None, table,
                                bass.IndirectOffsetOnAxis(ap=stage_i[:, h, c:c + 1], axis=0)
                            ).then_inc(s_land[h], 16)

            with pool.Fori(0, LOOPED) as it:
                for half in range(2):
                    iteration(it * 2 + (half + 1), table_d[1 - half])
            iteration(ITERATIONS - 1, table_d[1])
            for h in range(2):
                pool.wait_ge(s_resd[h], 16 * (NB // 2 + (1 if h == 0 else 0)))
            rounds(AW, x1_d, FIRST["final_put"], put=N)
            with pool.If(in_order == 0):
                rounds(C, edge_attr, 0, idx=s_idxb[1], land=s_landb[1])
            for h in range(2):
                pool.wait_ge(s_land[h], (FIRST["x1_get"] // 2) * LANDED)
            rounds(AW, x1_d, FIRST["x1_get"])
            pool.wait_ge(s_aggd, 16)
            rounds(C, agg_d, FIRST["agg_put"], put=N)

            def add_bias(h, np_, i):
                pool.wait_ge(s_x1in[h], i * 16 + 16)
                nc.gpsimd.tensor_tensor(d2[h]["x"][0:np_, :, 0:C], d2[h]["x"][0:np_, :, 0:C],
                                        bias_b[0:np_].unsqueeze(1).to_broadcast([np_, ROWS, C]),
                                        ALU.add).then_inc(s_biased, 1)

            pool.wait_ge(s_weights, 80)
            with pool.Fori(0, NB // BUFS) as i:
                for h in range(BUFS):
                    add_bias(h, P, i)
            add_bias(0, TAILP, NB // BUFS)

        @block.scalar
        def _(act):
            act.dma_start(src_d[0:E].rearrange("(p c) -> p c", p=80), src.rearrange("(p c) -> p c", p=80)).then_inc(s_srcd, 16)
            act.wait_ge(s_padt, 1)
            act.dma_start(src_d[E:SLOTS].rearrange("(o c) -> o c", o=1), pads[1:2, :]).then_inc(s_srcd, 16)
            act.dma_start(dst_d[0:E].rearrange("(p c) -> p c", p=80), dst.rearrange("(p c) -> p c", p=80)).then_inc(s_padded, 16)
            act.dma_start(dst_d[E:SLOTS].rearrange("(o c) -> o c", o=1), pads[0:1, :]).then_inc(s_padded, 16)
            act.dma_start(attr_d[0:E, :].rearrange("(p r) f -> p (r f)", p=400),
                          edge_attr.rearrange("(p r) f -> p (r f)", p=400)).then_inc(s_padded, 16)
            act.dma_start(attr_d[E:SLOTS, :].rearrange("(p r) f -> p (r f)", p=AP0Z), zeros[0:AP0Z]).then_inc(s_padded, 16)
            for k in range(QUAD):
                act.dma_start(wblk[k * C:(k + 1) * C, k * C:(k + 1) * C], weight).then_inc(s_weights, 16)
            act.dma_start(bias_b[:], bias.rearrange("(o f) -> o f", o=1).to_broadcast([P, C])).then_inc(s_weights, 16)
            quads = xrec_d.rearrange("(p c) f -> p c f", p=P)
            with act.Fori(0, PAIRS) as i:
                for h in range(2):
                    act.wait_ge(s_xland[h], i * LANDED + LANDED)
                    act.dma_start(quads[:, bass.ds((i * 2 + h) * (GC // QUAD), GC // QUAD), 0:QUAD * C],
                                  stage[:, h, 0:GC * C].rearrange("p (c f) -> p c f", f=QUAD * C)).then_inc(s_xrecd[h], 16)
            act.wait_ge(s_deg, 1)
            nc.scalar.activation(length[:], length[:], ACT.Sqrt).then_inc(s_degroot, 1)
            chunk = "(p r) f -> p (r f)"

            def load_chunk(k, lo):
                act.dma_start(x_in[k][0:XP].rearrange("p a b -> p (a b)"),
                              x[bass.ds(lo, XP * XR), :].rearrange(chunk, r=XR)).then_inc(s_xload[k], 16)

            def widen(k, i):
                act.wait_ge(s_xload[k], i * 16 + 16)
                nc.scalar.activation(x_wide[k][0:XP, :, 0:C], x_in[k][0:XP], ACT.Copy).then_inc(s_xmade, 1)
                nc.scalar.activation(x_wide[k][0:XP, :, C:AW],
                                     numbers[0:XP, bass.ds(i * 2 + k, 1)].rearrange("p o r -> p r o"),
                                     ACT.Copy).then_inc(s_xmade, 1)
                act.wait_ge(s_xmade, i * 4 + (2 * k + 3))
                act.dma_start(xmap_d[bass.ds(i * (2 * XP * XR) + k * (XP * XR), XP * XR), :].rearrange(chunk, r=XR),
                              x_wide[k][0:XP].rearrange("p a b -> p (a b)")).then_inc(s_xmapd[k], 16)

            for k in range(2):
                load_chunk(k, k * (XP * XR))
            act.wait_ge(s_numbers, 1)
            nc.scalar.activation(numbers[0:XP], numbers_i[0:XP], ACT.Copy).then_inc(s_xmade, 1)
            act.wait_ge(s_xmade, 1)
            for k in range(2):
                widen(k, 0)
            with act.Fori(1, CHUNKS // 2) as i:
                for k in range(2):
                    load_chunk(k, i * (2 * XP * XR) + k * (XP * XR))
                for k in range(2):
                    act.wait_ge(s_xmapd[k], i * 16)
                    widen(k, i)
            with act.Fori(0, PIECES) as i:
                piece = bass.ds(i * (N // PIECES), N // PIECES)
                for t in range(2):
                    act.dma_start(table_d[t][piece, :].rearrange("(p r) f -> p (r f)", r=PR),
                                  x[piece, :].rearrange("(p r) f -> p (r f)", r=PR)).then_inc(s_xcopy, 16)
                act.wait_ge(s_xcopy, i * 32 + 32)
            act.wait_ge(s_wsel, 1)
            nc.scalar.activation(wgt[:], wgt[:], ACT.Sqrt).then_inc(s_sqrt, 1)

            def root(h, np_, n):
                act.wait_ge(s_var, n)
                nc.scalar.activation(d1[h]["std"][0:np_], d1[h]["var"][0:np_], ACT.Sqrt, scale=1.0 / C,
                                     bias=small[0:np_, 0:1]).then_inc(s_std, 1)

            def store(h, np_, lo, n):
                act.wait_ge(s_res, n)
                act.dma_start(x1_d[bass.ds(lo, np_ * ROWS), :].rearrange("(p r) f -> p (r f)", r=ROWS),
                              d1[h]["o"][0:np_].rearrange("p a b -> p (a b)")).then_inc(s_resd[h], 16)

            def load_x(h, np_, lo):
                act.dma_start(d1[h]["y"][0:np_].rearrange("p a b -> p (a b)"),
                              x[bass.ds(lo, np_ * ROWS), :].rearrange("(p r) f -> p (r f)", r=ROWS)
                              ).then_inc(s_in[h], 16)

            act.wait_ge(s_go1, 1)
            for h in range(2):
                load_x(h, P, h * BLOCK)
            with act.Fori(1, NB // 2) as i:
                for h in range(2):
                    root(h, P, i * 2 + (h - 1))
                for h in range(2):
                    store(h, P, (i - 1) * (2 * BLOCK) + h * BLOCK, i * 2 + (h - 1))
                for h in range(2):
                    act.wait_ge(s_resd[h], i * 16)
                    load_x(h, P, i * (2 * BLOCK) + h * BLOCK)
            for h in range(2):
                root(h, P, NB + h - 1)
            for h in range(2):
                store(h, P, (NB - 2 + h) * BLOCK, NB + h - 1)
            act.wait_ge(s_resd[0], (NB // 2) * 16)
            load_x(0, TAILP, NB * BLOCK)
            root(0, TAILP, NB + 1)
            store(0, TAILP, NB * BLOCK, NB + 1)

            with act.Fori(0, NG) as g:
                act.wait_ge(s_nvar, g + 1)
                nc.scalar.activation(stats[:, 3], stats[:, 2], ACT.Sqrt, scale=1.0 / C,
                                     bias=small[:, 0:1]).then_inc(s_nstd, 1)

            act.sem_inc(s_sumc, 2)

            def turned_copy(h, np_, n):
                act.wait_ge(s_sumt, n + 1)
                act.wait_ge(s_mm, n + 1)
                nc.scalar.activation(turned_sum[h].rearrange("p (k n) -> p k n", k=QUAD)[:, :, 0:np_],
                                     ps_t[h % 2].rearrange("p (k n) -> p k n", k=QUAD)[:, :, 0:np_],
                                     ACT.Copy).then_inc(s_sumc, 1)

            def square_and_root(hs, np_, base):
                for h in hs:
                    act.wait_ge(s_centred, base + (h + 1))
                    nc.scalar.activation(d2[h]["sq"][0:np_], d2[h]["y"][0:np_], ACT.Square).then_inc(s_squared, 1)
                for h in hs:
                    act.wait_ge(s_lvar, base + (h + 1))
                    nc.scalar.activation(d2[h]["std"][0:np_], d2[h]["var"][0:np_], ACT.Sqrt, scale=1.0 / C,
                                         bias=small[0:np_, 0:1]).then_inc(s_lstd, 1)

            def store_results(hs, np_, base):
                for h in hs:
                    act.wait_ge(s_lres, base + (h + 1))
                    act.dma_start(out[bass.ds(base * BLOCK + h * BLOCK, np_ * ROWS), :]
                                  .rearrange("(p r) f -> p (r f)", r=ROWS),
                                  d2[h]["f"][0:np_].rearrange("p a b -> p (a b)")).then_inc(s_lresd[h], 16)

            every = range(BUFS)
            for h in every:
                turned_copy(h, P, h)
            with act.Fori(0, NB // BUFS - 1) as i:
                square_and_root(every, P, i * BUFS)
                for h in every:
                    turned_copy(h, P, i * BUFS + (BUFS + h))
                store_results(every, P, i * BUFS)
            square_and_root(every, P, NB - BUFS)
            turned_copy(0, TAILP, NB)
            store_results(every, P, NB - BUFS)
            square_and_root((0,), TAILP, NB)
            store_results((0,), TAILP, NB)

        @block.tensor
        def _(pe):
            pe.wait_ge(s_iota, 6)
            for r in range(7):
                for back in range(2):
                    source = turn_buf[(r + 1) % 2] if back else sort_buf[0]
                    target = turned_b if back else turned_a
                    pe.wait_ge(s_toturn, 2 * r + back + 1)
                    for b in range(W2 // P):
                        t = nc.tensor.transpose(target[:, b * P:(b + 1) * P], source[:, b * P:(b + 1) * P], ident[:])
                    t.then_inc(s_turned, 1)
            asked = Count(s_ask)

            def small_turn(out_, in_, wait=True):
                n_in = in_.shape[0]
                if wait:
                    asked.n += 1
                    pe.wait_ge(s_ask, asked.value())
                    pe.sem_inc(s_pegate, 1)
                return nc.tensor.transpose(out_, in_, ident[0:n_in, 0:n_in])

            for a in range(2):
                t = small_turn(ps_small[0:1, a * P:(a + 1) * P], small[:, 8 + a:9 + a], wait=a == 0)
            t.then_inc(s_ans, 1)
            for a in range(2):
                t = small_turn(ps_small[:, 2 * P + a:2 * P + a + 1], line[0:1, a, 0:P], wait=a == 0)
            t.then_inc(s_ans, 1)
            for m in range(2):
                t = small_turn(ps_small[0:1, m * P:(m + 1) * P], small[:, 10 + m:11 + m], wait=m == 0)
            t.then_inc(s_ans, 1)
            for m in range(3):
                t = small_turn(ps_small[0:C, m * P:(m + 1) * P], cross_col[:, m, :], wait=m == 0)
            t.then_inc(s_ans, 1)

            def carries(g, x_, w):
                small_turn(ps_small[0:C, 0:P], run_column(g, x_)).then_inc(s_ans, 1)
                small_turn(ps_small[:, 2 * P:2 * P + C], ends_t[:, w, w:w + P]).then_inc(s_ans, 1)

            with pe.Fori(0, ITERATIONS - 1) as it:
                start = asked.enter(it, 4)
                carries(NG - 1, GC, 0)
                carries(0, 1, 1)
                asked.leave(start, ITERATIONS - 1)
            carries(NG - 1, GC, 0)
            carries(NG - 1, GC, 0)

            def turn_sums(h, np_, n, i):
                pe.wait_ge(s_sumin[h], i * 16 + 16)
                pe.wait_ge(s_sumc, n + 1)
                for q in range(ROWS // QUAD):
                    tr = nc.tensor.transpose(ps_t[h % 2][:, q * P:q * P + np_],
                                             d2[h]["agg"][0:np_, q * QUAD:(q + 1) * QUAD].rearrange("p a b -> p (a b)"),
                                             ident[0:np_, 0:np_])
                tr.then_inc(s_sumt, 1)

            def multiply(h, np_, n):
                pe.wait_ge(s_mmfree, n + 1)
                pe.wait_ge(s_sumc, n + 3)
                for q in range(ROWS // QUAD):
                    mm = nc.tensor.matmul(ps_y[h][0:np_, q * P:(q + 1) * P], turned_sum[h][:, q * P:q * P + np_],
                                          wblk[:], start=True, stop=True)
                mm.then_inc(s_mm, 1)

            pe.wait_ge(s_weights, 80)
            pe.sem_inc(s_mm, BUFS)
            with pe.Fori(0, NB // BUFS) as i:
                turn_sums(0, P, i * BUFS, i)
                for h in range(1, BUFS):
                    turn_sums(h, P, i * BUFS + h, i)
                    multiply(h - 1, P, i * BUFS + (h - 1))
                multiply(BUFS - 1, P, i * BUFS + (BUFS - 1))
            turn_sums(0, TAILP, NB, NB // BUFS)
            multiply(0, TAILP, NB)

        @block.vector
        def _(v):
            V = nc.vector
            done = Count(s_dve)

            def settle():
                v.sem_inc(s_settled, 1)

            def step(instruction):
                done.inc(instruction)
                v.wait_ge(s_dve, done.value())

            def put_indices(tile, g, h):
                step(V.tensor_scalar(stage_i[:, h, :], tile[:, bass.ds(g * GC, GC)], 0, None, ALU.add))

            step(V.memset(small[:, 0:1], EPS))
            step(V.memset(zero_i[:], 0))
            step(V.memset(ends_t[:], 0.0))
            step(V.memset(line, 0.0))
            step(V.memset(wblk[:], 0.0))
            for r in range(QUAD):
                step(V.memset(four[:, r:r + 1], float(r)))
            step(V.memset(match[:], 0.0))
            v.sem_inc(s_mmfree, BUFS)
            step(V.memset(zeros, 0.0))
            step(V.memset(pads[:], 0))
            step(V.memset(pads[0:1, :], N))
            v.sem_inc(s_padt, 1)
            v.wait_ge(s_edges, 48)
            v.wait_ge(s_iota, 5)
            for a in range(2):
                step(V.tensor_copy(rec[0:ER, :, a, :], raw_edges[0:ER, a, :].rearrange("p (c q) -> p c q", q=QUAD)))
            step(V.tensor_copy(rec[0:ER, :, 2, :], raw_w[0:ER].bitcast(I32).rearrange("p (c q) -> p c q", q=QUAD)))
            v.sem_inc(s_quads, 1)
            key_i = sort_buf[0].bitcast(I32)
            key_e = key_i.rearrange("p (a c) -> p a c", a=2)[0:ER, :, 0:EC]
            step(V.tensor_scalar(key_e, raw_edges[0:ER], KEY_OFFSET, None, ALU.add))
            step(V.tensor_scalar(key_i, key_i, KEY_SHIFT, None, ALU.logical_shift_left))
            step(V.tensor_tensor(key_e, key_e, quarter[0:ER].unsqueeze(1).to_broadcast([ER, 2, EC]), ALU.bitwise_or))

            for b in range(7):
                step(V.tensor_scalar(small_i[:, 1:2], small_i[:, 0:1], b, None, ALU.logical_shift_right))
                step(V.tensor_scalar(small_i[:, 1:2], small_i[:, 1:2], 1, None, ALU.bitwise_and))
                step(V.tensor_scalar(small[:, 16 + b:17 + b], small_i[:, 1:2], -2.0, 1.0, ALU.mult, ALU.add))
            step(V.tensor_tensor(small[:, 24:30], small[:, 16:22], small[:, 17:23], ALU.mult))

            def compare(target, source, bit):
                s = source.rearrange("p (a h b) -> p a h b", h=2, b=1 << bit)
                t = target.rearrange("p (a h b) -> p a h b", h=2, b=1 << bit)
                done.inc(V.tensor_tensor(t[:, :, 0, :], s[:, :, 0, :], s[:, :, 1, :], ALU.min))
                step(V.tensor_tensor(t[:, :, 1, :], s[:, :, 0, :], s[:, :, 1, :], ALU.max))

            def flip(buf, bit):
                s = buf.rearrange("p (a h b) -> p a h b", h=2, b=1 << bit)
                step(V.tensor_scalar(s[:, :, 1, :], s[:, :, 1, :], -1.0, None, ALU.mult))

            SIDE_BITS = 9
            at = 0
            for k in range(1, SIDE_BITS + 1):
                if k < SIDE_BITS:
                    flip(sort_buf[at], k)
                else:
                    step(V.tensor_scalar(sort_buf[at], sort_buf[at], small[:, 16:17], None, ALU.mult))
                for j in reversed(range(k)):
                    compare(sort_buf[1 - at], sort_buf[at], j)
                    at = 1 - at
                if k < SIDE_BITS:
                    flip(sort_buf[at], k)
            for r in range(7):
                sign = small[:, 24 + r:25 + r] if r < 6 else small[:, 22:23]
                step(V.tensor_scalar(sort_buf[0], sort_buf[at], sign, None, ALU.mult))
                v.sem_inc(s_toturn, 1)
                v.wait_ge(s_turned, 2 * r + 1)
                step(V.tensor_copy(turn_buf[0], turned_a[:]))
                turn = 0
                for j in reversed(range(r + 1)):
                    compare(turn_buf[1 - turn], turn_buf[turn], j)
                    turn = 1 - turn
                v.sem_inc(s_toturn, 1)
                v.wait_ge(s_turned, 2 * r + 2)
                step(V.tensor_copy(sort_buf[1], turned_b[:]))
                at = 1
                for j in reversed(range(SIDE_BITS)):
                    compare(sort_buf[1 - at], sort_buf[at], j)
                    at = 1 - at
            v.sem_inc(s_sorted, 1)

            v.wait_ge(s_keys, 32)
            own = slice(LEAD, LEAD + COLS)
            node_i = part(window, 0, [2 * KW], I32).rearrange("p (a c) -> p a c", a=2)
            step(V.tensor_scalar(quad[:], keys[:, :, own], (1 << KEY_SHIFT) - 1, None, ALU.bitwise_and))
            for h in range(2):
                put_indices(quad[:, 0], h, h)
                v.sem_inc(s_idx, 1)
            step(V.tensor_scalar(node_i, keys[:], KEY_SHIFT, None, ALU.logical_shift_right))
            step(V.tensor_scalar(node[:], node_i, -KEY_OFFSET, None, ALU.add))
            keyf = keys[:].bitcast(F32)

            def before(t, d):
                return t[:, :, LEAD - d:LEAD - d + COLS]

            step(V.tensor_tensor(twin[:], keyf[:, :, own], before(keyf, 1), ALU.is_equal))
            for d in (2, 3):
                step(V.tensor_tensor(same[:], keyf[:, :, own], before(keyf, d), ALU.is_equal))
                step(V.tensor_tensor(twin[:], twin[:], same[:], ALU.add))
            step(V.tensor_tensor(same[:], node[:, :, own], before(node, 1), ALU.is_equal))
            slot_f = diff[:].rearrange("p c f -> p (c f)")[:, 0:COLS]
            head = diff[:].rearrange("p c f -> p (c f)")[:, COLS:2 * COLS]
            step(V.tensor_copy(slot_f, slot_i[:]))
            for a in range(2):
                step(V.tensor_scalar(head, same[:, a], -1.0, 1.0, ALU.mult, ALU.add))
                step(V.tensor_tensor(head, head, slot_f, ALU.mult))
                step(v.tensor_tensor_scan(length[:, a], head, head, 0.0, ALU.max, ALU.max))
                step(V.tensor_copy(small[:, 8 + a:9 + a], length[:, a, COLS - 1:COLS]))
            asks = Count(s_ask)
            answers = Count(s_ans)

            def ask():
                asks.n += 1
                v.sem_inc(s_ask, 1)
                answers.n += 1
                v.wait_ge(s_ans, answers.value())

            ask()
            for a in range(2):
                step(V.tensor_copy(line[0:1, 2 + a, 0:P], ps_small[0:1, a * P:(a + 1) * P]))
                step(v.tensor_tensor_scan(line[0:1, a, 1:P + 1], line[0:1, 2 + a, 0:P], line[0:1, 2 + a, 0:P], 0.0,
                                          ALU.max, ALU.max))
            ask()
            step(V.tensor_copy(small[:, 8:10], ps_small[:, 2 * P:2 * P + 2]))
            for a in range(2):
                step(V.tensor_scalar(length[:, a], length[:, a], small[:, 8 + a:9 + a], None, ALU.max))
                step(V.tensor_tensor(length[:, a], slot_f, length[:, a], ALU.subtract))
            step(V.tensor_scalar(length[:], length[:], 1.0, None, ALU.add))
            step(V.tensor_reduce(small[:, 10:11], length[:].rearrange("p a c -> p (a c)"), AX.X, ALU.max))
            v.wait_ge(s_dsts, 16)
            step(V.tensor_scalar(same[:, 0], node[:, 1, own], float(N), None, ALU.min))
            step(V.tensor_tensor(same[:, 0], same[:, 0], dst_slots, ALU.is_equal))
            step(V.tensor_reduce(small[:, 11:12], same[:, 0], AX.X, ALU.min))
            ask()
            step(V.tensor_reduce(flags[:, 0:1], ps_small[0:1, 0:P], AX.X, ALU.max))
            step(V.tensor_reduce(flags[:, 1:2], ps_small[0:1, P:2 * P], AX.X, ALU.min))
            v.sem_inc(s_flags, 1)
            v.sem_inc(s_deg, 1)
            lastf = part(window, 0, [2 * COLS]).rearrange("p (a c) -> p a c", a=2)
            step(V.tensor_tensor(lastf, node[:, :, own], node[:, :, LEAD + 1:LEAD + 1 + COLS], ALU.is_equal))
            step(V.scalar_tensor_tensor(last_i[:], lastf, float(1 << 20), node[:, :, own], ALU.mult, ALU.add))
            step(V.memset(cross[:], 0.0))
            for m, (a, at_, scale) in enumerate(((0, LEAD - 1, BIG), (0, LEAD + COLS, BIG), (1, LEAD - 1, 1.0))):
                step(V.tensor_scalar(cross[:, m, 1:], node[:, a, own], node[:, a, at_:at_ + 1], scale,
                                     ALU.is_equal, ALU.mult))
                far = 1 if m == 1 else COLS
                step(V.tensor_copy(cross_col[:, m, :], cross[:, m, far:far + 1].to_broadcast([P, C])))
            ask()
            step(V.tensor_copy(whole[:].rearrange("c m p -> c (m p)"), ps_small[0:C, 0:3 * P]))
            long_runs = v.value_load(flags[0:1, 0:1], min_val=0, max_val=SLOTS) > NEAR
            in_order = v.value_load(flags[0:1, 1:2], min_val=0, max_val=1)
            v.wait_ge(s_degroot, 1)
            step(V.reciprocal(length[:], length[:]))

            def window_of(tile, g):
                return tile[:, bass.ds(g * FLAT, FLAT)].rearrange("p (f w) -> p f w", w=WIN)

            def build_mask(g, a, scale):
                step(V.tensor_tensor(stats[:, 0], node[:, a, bass.ds(g * GC + LEAD, GC)],
                                     node[:, a, bass.ds(g * GC + (LEAD - 1), GC)], ALU.is_equal))
                step(V.tensor_scalar(window_of(joined, g)[:, :, 1:],
                                     stats[:, 0].unsqueeze(1).to_broadcast([P, C, GC]), scale, None, ALU.mult))


            def masks(a, scale):
                def beside(i):
                    for h in range(2):
                        build_mask(i * 2 + h, a, scale)
                return beside

            def one_pass(first, fill, consume, steps, fills, beside=None, beside_steps=0, idx=s_idx, land=s_land,
                         begun=False):
                if not begun:
                    for h in range(2):
                        fill(h, h, 0)
                        v.sem_inc(idx, 1)
                settle()
                with v.Fori(0, PAIRS - 1) as i:
                    start = done.enter(i, 2 * (steps + fills) + beside_steps)
                    for h in range(2):
                        v.wait_ge(land[h], i * LANDED + (first // 2 + 1) * LANDED)
                        consume(i * 2 + h, h)
                        fill(i * 2 + (h + 2), h, i + 1)
                        v.sem_inc(idx, 1)
                    if beside:
                        beside(i)
                    settle()
                    done.leave(start, PAIRS - 1)
                for h in range(2):
                    v.wait_ge(land[h], (first // 2 + PAIRS) * LANDED)
                    consume(NG - 2 + h, h)

            def otherwise(condition, general, else_, steps):
                before = done.n
                settle()
                with v.If(condition):
                    general()
                    settle()
                with v.Else():
                    else_()
                    v.sem_inc(s_dve, steps)
                assert done.n - before == steps, (done.n - before, steps)
                v.wait_ge(s_dve, done.value())

            def group(tile, g):
                return tile[..., bass.ds(g * GC, GC)]

            def select(a, wanted):
                def consume(g, h):
                    if a == 0:
                        wide = stage_x[h].rearrange("p (c w) -> p c w", w=XREC)
                        x4 = wide[:, :, 0:QUAD * C].rearrange("p c (q f) -> p c q f", q=QUAD)
                        rec4 = wide[:, :, QUAD * C:XREC].bitcast(I32).rearrange("p c (k q) -> p c k q", k=3)
                    else:
                        rec4 = stage[:, h, 0:GC * 3 * QUAD].bitcast(I32).rearrange("p (c k q) -> p c k q", k=3, q=QUAD)
                    m, cnt, sel, prod = (match[:, k] for k in range(4))
                    step(V.tensor_tensor(m, rec4[:, :, a, :], node[:, a, bass.ds(g * GC + LEAD, GC)].unsqueeze(2)
                                         .to_broadcast([P, GC, QUAD]), ALU.is_equal))
                    step(V.tensor_scalar(cnt[:, :, 1:2], m[:, :, 0:1], 1.0, None, ALU.mult))
                    step(V.tensor_tensor(cnt[:, :, 2:3], cnt[:, :, 1:2], m[:, :, 1:2], ALU.add))
                    step(V.tensor_tensor(cnt[:, :, 3:4], cnt[:, :, 2:3], m[:, :, 2:3], ALU.add))
                    step(V.tensor_tensor(sel, cnt, twin[:, a, bass.ds(g * GC, GC)].unsqueeze(2)
                                         .to_broadcast([P, GC, QUAD]), ALU.is_equal))
                    step(V.tensor_tensor(sel, sel, m, ALU.mult))
                    for values, target in wanted(rec4, g):
                        step(V.tensor_tensor(prod, sel, values, ALU.mult))
                        step(V.tensor_tensor(prod[:, :, 0:2], prod[:, :, 0:2], prod[:, :, 2:4], ALU.add))
                        step(V.tensor_tensor(target, prod[:, :, 0:1], prod[:, :, 1:2], ALU.add))
                    if a == 0:
                        step(V.tensor_tensor(x4, x4, sel.unsqueeze(3).to_broadcast([P, GC, QUAD, C]), ALU.mult))
                        step(V.tensor_tensor(x4[:, :, 0:2], x4[:, :, 0:2], x4[:, :, 2:4], ALU.add))
                        step(V.tensor_tensor(tbuf[:, h], x4[:, :, 0], x4[:, :, 1], ALU.add))
                        v.sem_inc(s_rows, 1)
                return consume

            def of_a(rec4, g):
                return ((rec4[:, :, 1, :], other[:, 0, bass.ds(g * GC, GC)].unsqueeze(2)),
                        (rec4[:, :, 2, :].bitcast(F32), wgt[:, bass.ds(g * GC, GC)].unsqueeze(2)))

            def of_b(rec4, g):
                return ((rec4[:, :, 0, :], other[:, 1, bass.ds(g * GC, GC)].unsqueeze(2)),
                        (four[:].unsqueeze(1).to_broadcast([P, GC, QUAD]),
                         edge_b[:, bass.ds(g * GC, GC)].unsqueeze(2)))

            def rows_kept(i):
                for h in range(2):
                    v.wait_ge(s_tabled[h], i * 16 + 16)

            one_pass(FIRST["rec_a"], lambda g, h, i: put_indices(quad[:, 0], g, h), select(0, of_a), 15, 1,
                     rows_kept, 0, begun=True)
            v.sem_inc(s_wsel, 1)
            def find_b():
                one_pass(0, lambda g, h, i: put_indices(quad[:, 1], g, h), select(1, of_b), 12, 1,
                         idx=s_idxb[0], land=s_landb[0])
                step(V.scalar_tensor_tensor(edge_b[:], quad[:, 1], float(QUAD), edge_b[:], ALU.mult, ALU.add))

            def wait_b():
                v.wait_ge(s_srcin, 16)
                settle()

            otherwise(in_order == 0, find_b, wait_b, 13 * NG + 1)
            v.sem_inc(s_rowsfree, 1)

            def fill_map(g, h, i):
                step(V.tensor_scalar(stage[:, h, 0:GC], slot_i[:, bass.ds(g * GC, GC)], float(N), None, ALU.add))
                step(V.tensor_scalar(stage_i[:, h, :], last_i[:, 0, bass.ds(g * GC, GC)], float(AW), float(C),
                                     ALU.mult, ALU.add))

            def norm_steps(u, np_, target, n):
                def bc(a):
                    return a[0:np_].unsqueeze(2).to_broadcast([np_, ROWS, C])
                def centre():
                    step(V.tensor_reduce(u["sum"][0:np_], u["y"][0:np_], AX.X, ALU.add))
                    step(V.tensor_scalar(u["mean"][0:np_], u["sum"][0:np_], 1.0 / C, None, ALU.mult))
                    step(V.tensor_tensor(u["y"][0:np_], u["y"][0:np_], bc(u["mean"]), ALU.subtract))
                    step(V.tensor_tensor(u["sq"][0:np_], u["y"][0:np_], u["y"][0:np_], ALU.mult))
                    step(V.tensor_reduce(u["var"][0:np_], u["sq"][0:np_], AX.X, ALU.add))
                    v.sem_inc(s_var, 1)
                def norm():
                    v.wait_ge(s_std, n)
                    step(V.reciprocal(u["rstd"][0:np_], u["std"][0:np_]))
                    step(V.tensor_tensor(target, u["y"][0:np_], bc(u["rstd"]), ALU.mult))
                    v.sem_inc(s_res, 1)
                return centre, norm

            for h in range(2):
                step(V.memset(d1[h]["o"][:, :, C:AW], 1.0))
            v.sem_inc(s_go1, 1)

            def x_blocks(n, np_, hs):
                parts = []
                for h in hs:
                    u = d1[h]
                    v.wait_ge(s_in[h], n * 16 + 16)
                    step(V.tensor_scalar(u["y"][0:np_], u["y"][0:np_], 2.0, None, ALU.mult))
                    parts.append(norm_steps(u, np_, u["o"][0:np_, :, 0:C], n * 2 + (h + 1)))
                    parts[-1][0]()
                for _, norm in parts:
                    norm()

            BLOCK_PAIRS = NB // 2 // (PAIRS - 1)
            assert NB // 2 == (PAIRS - 1) * BLOCK_PAIRS

            def masks_and_x(i):
                masks(0, BIG)(i)
                for j in range(BLOCK_PAIRS):
                    x_blocks(i * BLOCK_PAIRS + j, P, (0, 1))

            for h in range(2):
                fill_map(h, h, 0)
                v.sem_inc(s_idx, 1)
            step(V.memset(joined[:], 0.0))
            one_pass(FIRST["map_put"], fill_map, lambda g, h: None, 0, 2, masks_and_x, 4 + 2 * 8 * BLOCK_PAIRS,
                     begun=True)
            masks(0, BIG)(PAIRS - 1)

            def stage_rows(h):
                return stage[:, h, 0:GC * C].rearrange("p (c f) -> p c f", f=C)

            def rows_of(g):
                return rows[:, bass.ds(g, 1)].rearrange("p o c f -> p (o c) f")

            x_blocks(NB // 2, TAILP, (0,))

            win = window[:].rearrange("p (f w) -> p f w", w=WIN)

            def carry_in(g):
                step(V.tensor_scalar(win[:, :, 0:1],
                                     runs[:, bass.ds(g * FLAT, FLAT)].rearrange("p (f w) -> p f w", w=WIN)[:, :, GC:WIN],
                                     1.0, None, ALU.mult))

            def scan_forward(g, op0, op1):
                step(v.tensor_tensor_scan(runs[:, bass.ds(g * FLAT + FLAT, FLAT)], joined[:, bass.ds(g * FLAT, FLAT)],
                                          window[:], 0.0, op0, op1))

            def stage_wide(h):
                return stage[:, h, :].rearrange("p (c f) -> p c f", f=AW)

            def rises(g, destinations):
                step(V.tensor_tensor(diff[:], destinations, rows_of(g), ALU.subtract))
                carry_in(g)
                step(V.scalar_tensor_tensor(win[:, :, 1:].rearrange("p f c -> p c f"), diff[:], 0.0,
                                            wgt[:, bass.ds(g * GC, GC)].unsqueeze(2).to_broadcast([P, GC, C]),
                                            ALU.max, ALU.mult))
                scan_forward(g, ALU.min, ALU.max)

            def run_win(g):
                return runs[:, bass.ds(g * FLAT + FLAT, FLAT)].rearrange("p (f w) -> p f w", w=WIN)

            def apply(g, m, w0, w1, op0, op1):
                n = w1 - w0
                step(V.tensor_tensor(fix[:, :, 0:n],
                                     cross[:, m, bass.ds(g * GC + w0, n)].unsqueeze(1).to_broadcast([P, C, n]),
                                     ps_small[:, 2 * P:2 * P + C].unsqueeze(2).to_broadcast([P, C, n]), op0))
                step(V.tensor_tensor(run_win(g)[:, :, w0:w1], run_win(g)[:, :, w0:w1], fix[:, :, 0:n], op1))

            def over_partitions(m, backward, op0, op1):
                ask()
                if backward:
                    step(v.tensor_tensor_scan(ends_t[:, 1, 0:P][:, ::-1],
                                              whole[:, m, ::-1], ps_small[0:C, 0:P][:, ::-1], 0.0, op0, op1))
                else:
                    step(v.tensor_tensor_scan(ends_t[:, 0, 1:P + 1], whole[:, m, :], ps_small[0:C, 0:P], 0.0, op0, op1))
                ask()
                if backward:
                    near, far = (NG - 1, WIN - NEAR, WIN), (NG - 1, 1, WIN - NEAR)
                    rest, w0 = (0, NG - 1), 1
                else:
                    near, far = (0, 1, 1 + NEAR), (0, 1 + NEAR, WIN)
                    rest, w0 = (1, NG), 0
                apply(near[0], m, near[1], near[2], op0, op1)
                before_if = done.n
                far_steps = 2 + 2 * (rest[1] - rest[0])
                settle()
                with v.If(long_runs):
                    apply(far[0], m, far[1], far[2], op0, op1)
                    settle()
                    with v.Fori(0, rest[1] - rest[0]) as g:
                        start = done.enter(g, 2)
                        apply(g + rest[0], m, w0, WIN, op0, op1)
                        settle()
                        done.leave(start, rest[1] - rest[0])
                with v.Else():
                    v.sem_inc(s_dve, far_steps)
                assert done.n - before_if == far_steps
                v.wait_ge(s_dve, done.value())

            def scan_backward(g):
                at = (g + 1) * FLAT
                step(v.tensor_tensor_scan(runs[:, at:at + FLAT][:, ::-1], joined[:, g * FLAT + 1:(g + 1) * FLAT + 1][:, ::-1],
                                          runs[:, at:at + FLAT][:, ::-1], 0.0, ALU.min, ALU.max))

            def new_rows(target, g, cols=GC):
                step(V.tensor_tensor(target, rows_of(g)[:, 0:cols], run_win(g)[:, :, 1:1 + cols]
                                     .rearrange("p f c -> p c f"), ALU.add))

            v.wait_ge(s_sqrt, 1)
            for h in range(2):
                v.wait_ge(s_resd[h], 16 * (NB // 2 + (1 if h == 0 else 0)))
            v.wait_ge(s_rowsin, 16)
            step(V.memset(runs[:, 0:FLAT], 0.0))
            for h in range(2):
                put_indices(other[:, 0], h, h)
                v.sem_inc(s_idx, 1)

            def gathered(k, first=False, last=False):
                def pair(i, ahead):
                    for h in range(2):
                        g = i * 2 + h
                        v.wait_ge(s_land[h], k * (PAIRS * LANDED) + i * LANDED + (FIRST["round"] // 2 + 1) * LANDED)
                        rises(g, stage_wide(h)[:, :, 0:C] if first else stage_rows(h))
                        if first:
                            step(V.tensor_copy(gidx[:, bass.ds(g * GC, GC)].unsqueeze(2), stage_wide(h)[:, :, C:AW]))
                        if ahead:
                            put_indices(ahead, g + 2, h)
                        elif first:
                            put_indices(gidx, h, h)
                        if ahead or first:
                            v.sem_inc(s_idx, 1)
                        if not last:
                            v.wait_ge(s_tabled[h], k * (PAIRS * 16) + i * 16 + PAIRS * 16)
                            new_rows(tbuf[:, h], g)
                            v.sem_inc(s_table, 1)

                peeled = first or last
                pairs = PAIRS - 1 if peeled else PAIRS
                ahead = other[:, 0] if first else gidx
                settle()
                with v.Fori(0, pairs) as i:
                    inner = done.enter(i, 2 * (4 + 1 + (0 if last else 1) + (1 if first else 0)))
                    pair(i, ahead)
                    settle()
                    done.leave(inner, pairs)
                if peeled:
                    pair(PAIRS - 1, None)
                if first:
                    step(V.tensor_copy(gidx[:, COLS:COLS + 2 * GC], gidx[:, 0:2 * GC]))
                over_partitions(0, False, ALU.min, ALU.max)

            def iteration(k, first=False):
                gathered(k, first)

                def store_again():
                    for h in range(2):
                        v.wait_ge(s_tabled[h], k * (PAIRS * 16) + 2 * PAIRS * 16)
                    settle()
                    with v.Fori(0, NG) as g:
                        inner = done.enter(g, 1)
                        new_rows(tbuf[:, 0], g)
                        v.sem_inc(s_again, 1)
                        v.wait_ge(s_againd, k * (NG * 16) + g * 16 + 16)
                        settle()
                        done.leave(inner, NG)

                otherwise(long_runs, store_again, lambda: None, NG)
                v.wait_ge(s_tabled[0], k * (PAIRS * 16) + 2 * PAIRS * 16)
                if not first:
                    v.wait_ge(s_neard, k * 16)
                new_rows(near_rows[:], 0, NEAR)
                v.sem_inc(s_near, 1)
                scan_backward(NG - 1)
                for g in reversed(range(NG - 1)):
                    step(V.tensor_scalar(run_win(g)[:, :, GC:WIN], run_win(g + 1)[:, :, 0:1], 1.0, None, ALU.mult))
                    scan_backward(g)
                over_partitions(1, True, ALU.min, ALU.max)
                settle()
                with v.Fori(0, NG) as g:
                    inner = done.enter(g, 1)
                    new_rows(rows_of(g), g)
                    settle()
                    done.leave(inner, NG)

            iteration(0, first=True)
            settle()
            with v.Fori(0, LOOPED) as it:
                per = 2 * (NG * 6 + (3 + 2 * NG) + NG + 1 + (1 + 2 * (NG - 1)) + (3 + 2 * NG) + NG)
                start = done.enter(it, per)
                astart, bstart = asks.enter(it, 8), answers.enter(it, 8)
                for half in range(2):
                    iteration(it * 2 + (half + 1))
                settle()
                done.leave(start, LOOPED)
                asks.leave(astart, LOOPED)
                answers.leave(bstart, LOOPED)
            for h in range(2):
                v.wait_ge(s_tabled[h], 16 * PAIRS * ITERATIONS)
            v.sem_inc(s_xfree, 2)
            gathered(ITERATIONS - 1, last=True)

            square = window[:, 0:GC * C].rearrange("p (c f) -> p c f", f=C)

            def bcg(k):
                return stats[:, k].unsqueeze(2).to_broadcast([P, GC, C])

            def fill_norm(g, h, i):
                v.wait_ge(s_xin[h], i * 16 + 16)
                new_rows(diff[:], g)
                step(V.tensor_tensor(diff[:], tbuf[:, h], diff[:], ALU.add))
                v.sem_inc(s_xfree, 1)
                step(V.tensor_reduce(stats[:, 0], diff[:], AX.X, ALU.add))
                step(V.tensor_scalar(stats[:, 1], stats[:, 0], 1.0 / C, None, ALU.mult))
                step(V.tensor_tensor(diff[:], diff[:], bcg(1), ALU.subtract))
                step(V.tensor_tensor(square, diff[:], diff[:], ALU.mult))
                step(V.tensor_reduce(stats[:, 2], square, AX.X, ALU.add))
                v.sem_inc(s_nvar, 1)
                v.wait_ge(s_nstd, g + 1)
                step(V.reciprocal(stats[:, 4], stats[:, 3]))
                step(V.tensor_tensor(stage_wide(h)[:, :, 0:C], diff[:], bcg(4), ALU.mult))
                step(V.tensor_scalar(stage_wide(h)[:, :, C:AW], length[:, 0, bass.ds(g * GC, GC)].unsqueeze(2),
                                     1.0, None, ALU.mult))
                put_indices(last_i[:, 0], g, h)

            one_pass(FIRST["final_put"], fill_norm, lambda g, h: None, 0, 11,
                     masks(1, 1.0), 4)
            masks(1, 1.0)(PAIRS - 1)
            def take_attr(g, h):
                step(V.tensor_scalar(rows_of(g), stage_rows(h), 1.0, None, ALU.mult))

            def gather_attr():
                one_pass(0, lambda g, h, i: put_indices(edge_b, g, h), take_attr, 1, 1,
                         idx=s_idxb[1], land=s_landb[1])

            def wait_attr():
                v.wait_ge(s_attrin, 16)
                settle()

            v.sem_inc(s_free, 1)
            otherwise(in_order == 0, gather_attr, wait_attr, 2 * NG)

            def messages(g, h):
                carry_in(g)
                step(V.tensor_tensor(diff[:], stage_wide(h)[:, :, 0:C],
                                     stage_wide(h)[:, :, C:AW].to_broadcast([P, GC, C]), ALU.mult))
                step(V.tensor_tensor(win[:, :, 1:].rearrange("p f c -> p c f"), diff[:], rows_of(g), ALU.add))
                scan_forward(g, ALU.mult, ALU.add)

            one_pass(FIRST["x1_get"], lambda g, h, i: put_indices(other[:, 1], g, h), messages, 4, 1)
            over_partitions(2, False, ALU.mult, ALU.add)

            def fill_sums(g, h, i):
                step(V.tensor_tensor(stage_rows(h), run_win(g)[:, :, 1:].rearrange("p f c -> p c f"),
                                     length[:, 1, bass.ds(g * GC, GC)].unsqueeze(2).to_broadcast([P, GC, C]), ALU.mult))
                put_indices(last_i[:, 1], g, h)

            one_pass(FIRST["agg_put"], fill_sums, lambda g, h: None, 0, 2)
            v.sem_inc(s_go2, 1)

            def each(hs, instruction, after=None):
                ends = {}
                for h in hs:
                    if after:
                        v.wait_ge(s_dve, after[h])
                    done.inc(instruction(d2[h], h))
                    ends[h] = done.value()
                return ends

            def blocks(i, np_, hs):
                def bc(a):
                    return a[0:np_].unsqueeze(2).to_broadcast([np_, ROWS, C])

                if i is not FIRST_BLOCKS:
                    v.wait_ge(s_lres, i * BUFS)

                def add(u, h):
                    v.wait_ge(s_biased, i * BUFS + (h + 1))
                    v.wait_ge(s_mm, i * BUFS + (BUFS + h + 1))
                    return V.tensor_tensor(u["y"][0:np_], ps_y[h][0:np_].rearrange("p (r f) -> p r f", f=C),
                                           u["x"][0:np_, :, 0:C], ALU.add)
                ends = each(hs, add)
                ends = each(hs, lambda u, h: V.tensor_reduce(u["sum"][0:np_], u["y"][0:np_], AX.X, ALU.add), ends)
                v.sem_inc(s_mmfree, len(hs))
                ends = each(hs, lambda u, h: V.tensor_scalar(u["mean"][0:np_], u["sum"][0:np_], 1.0 / C, None,
                                                             ALU.mult), ends)
                for h in hs:
                    u = d2[h]
                    v.wait_ge(s_dve, ends[h])
                    V.tensor_tensor(u["y"][0:np_], u["y"][0:np_], bc(u["mean"]), ALU.subtract).then_inc(s_centred, 1)
                for h in hs:
                    u = d2[h]
                    v.wait_ge(s_squared, i * BUFS + (h + 1))
                    V.tensor_reduce(u["var"][0:np_], u["sq"][0:np_], AX.X, ALU.add).then_inc(s_lvar, 1)

                def invert(u, h):
                    v.wait_ge(s_lstd, i * BUFS + (h + 1))
                    return V.reciprocal(u["rstd"][0:np_], u["std"][0:np_])
                ends = each(hs, invert)
                for h in hs:
                    u = d2[h]
                    v.wait_ge(s_dve, ends[h])
                    if i is not FIRST_BLOCKS:
                        v.wait_ge(s_lresd[h], i * 16)
                    V.tensor_tensor(u["f"][0:np_], u["y"][0:np_], bc(u["rstd"]), ALU.mult).then_inc(s_lres, 1)

            FIRST_BLOCKS = 0
            blocks(FIRST_BLOCKS, P, range(BUFS))
            settle()
            with v.Fori(0, NB // BUFS - 1) as i:
                start = done.enter(i, BUFS * 4)
                blocks(i + 1, P, range(BUFS))
                settle()
                done.leave(start, NB // BUFS - 1)
            blocks(NB // BUFS, TAILP, (0,))


_INS = ["x", "src", "dst", "edge_attr_32", "edge_weight", "L1_gnn_weight", "L1_gnn_bias"]


def kernel(**inputs):
    import numpy as _np
    import concourse.bacc as _bacc
    from concourse import mybir as _mybir
    from concourse.bass_utils import run_bass_kernel_spmd as _run

    nc = _bacc.Bacc("TRN2", target_bir_lowering=False, num_devices=1)
    arrays, args = {}, []
    for name in _INS:
        a = _np.ascontiguousarray(inputs[name])
        arrays[f"in_{name}_dram"] = a
        args.append(nc.dram_tensor(f"in_{name}_dram", a.shape, _mybir.dt.from_np(a.dtype), kind="ExternalInput").ap())
    shape = arrays["in_x_dram"].shape
    args.append(nc.dram_tensor("out_0_dram", shape, _mybir.dt.float32, kind="ExternalOutput").ap())
    resnorm_gnn(nc, *args)
    r = _run(nc, [arrays], core_ids=[0])
    return r.results[0]["out_0_dram"]
```
